# Optimizing a Trainium2 kernel written in Bass

```python
import numpy as np
import jax
import jax.numpy as jnp

def _softmax(x, axis=-1):
    return jax.nn.softmax(x, axis=axis)

def _gelu(x):
    return jax.nn.gelu(x, approximate=True)

def _silu(x):
    return jax.nn.silu(x)

def _sigmoid(x):
    return jax.nn.sigmoid(x)

def _layernorm(x, axis=-1, eps=1e-05):
    m = jnp.mean(x, axis=axis, keepdims=True)
    v = jnp.var(x, axis=axis, keepdims=True)
    return (x - m) / jnp.sqrt(v + eps)

def _scatter_add(tgt, idx, src, axis=0):
    return tgt.at[idx].add(src)

def _segment_sum(src, seg, n):
    return jax.ops.segment_sum(src, seg, n)
kernel_name = 'mk_adj_preln_d2_adj_r2_7019ec'

def setup_inputs(seed: int=0):
    np.random.seed(seed)
    _w = jnp.asarray

    def _rec_inputs():
        import jax
        import jax.numpy as jnp
        _gk = jax.random.key(seed)
        x = -0.0002928 + 1 * jax.random.normal(jax.random.fold_in(_gk, 1), (16, 512, 256), jnp.float32)
        _w = (1.0 + jnp.arange(512, dtype=jnp.float32)) ** (-0.5)
        _w = _w / _w.mean()
        _pij = jnp.clip(0.0078125 * _w[:, None] * _w[None, :], 0.0, 1.0)
        _a = jax.random.uniform(jax.random.fold_in(_gk, 2), (16, 512, 512)) < _pij
        adj = _a.astype(jnp.int32)
        return (x, adj)
    x, adj = _rec_inputs()

    def _L0_gnn_setup():
        import jax, jax.numpy as jnp
        import numpy as np
        L = 3
        D = 256
        B, N = (8, 512)
        EPS = 1e-05

        def layernorm(x, gamma, beta):
            mu = jnp.mean(x, axis=-1, keepdims=True)
            var = jnp.var(x, axis=-1, keepdims=True)
            return (x - mu) * jax.lax.rsqrt(var + EPS) * gamma + beta
        key = jax.random.key(seed)
        ks = jax.random.split(key, 12)
        s = 1.0 / np.sqrt(D)
        node_features = jax.random.normal(ks[0], (B, N, D), dtype=jnp.float32)
        adjacency_matrix = jax.random.randint(ks[1], (B, N, N), 0, 2, dtype=jnp.int32)
        return {'node_features': node_features, 'adjacency_matrix': adjacency_matrix, 'attn_w': jax.random.normal(ks[2], (L, 2 * D), dtype=jnp.float32) * (1.0 / np.sqrt(2 * D)), 'attn_b': jax.random.normal(ks[3], (L,), dtype=jnp.float32) * 0.01, 'W1': jax.random.normal(ks[4], (L, D, 4 * D), dtype=jnp.float32) * s, 'b1': jnp.zeros((L, 4 * D), dtype=jnp.float32), 'W2': jax.random.normal(ks[5], (L, 4 * D, D), dtype=jnp.float32) * (1.0 / np.sqrt(4 * D)), 'b2': jnp.zeros((L, D), dtype=jnp.float32), 'g1': jnp.ones((L, D), dtype=jnp.float32), 'beta1': jnp.zeros((L, D), dtype=jnp.float32), 'g2': jnp.ones((L, D), dtype=jnp.float32), 'beta2': jnp.zeros((L, D), dtype=jnp.float32)}
    _L0_gnn_all = _L0_gnn_setup()
    _L0_gnn_in = {k: v for k, v in _L0_gnn_all.items() if k in ('attn_w', 'attn_b', 'W1', 'b1', 'W2', 'b2', 'g1', 'beta1', 'g2', 'beta2')}
    del _L0_gnn_all

    def _L1_gnn_setup():
        import jax, jax.numpy as jnp
        import numpy as np
        ALPHA = 0.2

        def _leaky(x):
            return jnp.where(x >= 0, x, ALPHA * x)
        key = jax.random.key(seed)
        k1, k2, k3, k4 = jax.random.split(key, 4)
        B, N, F_in, F_out = (4, 1024, 256, 256)
        h = jax.random.normal(k1, (B, N, F_in), dtype=jnp.float32)
        W = jax.random.normal(k2, (F_in, F_out), dtype=jnp.float32) * 0.05
        a = jax.random.normal(k3, (2 * F_out, 1), dtype=jnp.float32) * 0.05
        adj = jax.random.randint(k4, (B, N, N), 0, 2, dtype=jnp.int32)
        return {'h': h, 'W': W, 'a': a, 'adj': adj}
    _L1_gnn_all = _L1_gnn_setup()
    _L1_gnn_in = {k: v for k, v in _L1_gnn_all.items() if k in ('W', 'a')}
    del _L1_gnn_all
    return {'x': x, 'adj': adj, 'L0_gnn_attn_w': _L0_gnn_in['attn_w'], 'L0_gnn_attn_b': _L0_gnn_in['attn_b'], 'L0_gnn_W1': _L0_gnn_in['W1'], 'L0_gnn_b1': _L0_gnn_in['b1'], 'L0_gnn_W2': _L0_gnn_in['W2'], 'L0_gnn_b2': _L0_gnn_in['b2'], 'L0_gnn_g1': _L0_gnn_in['g1'], 'L0_gnn_beta1': _L0_gnn_in['beta1'], 'L0_gnn_g2': _L0_gnn_in['g2'], 'L0_gnn_beta2': _L0_gnn_in['beta2'], 'L1_gnn_W': _L1_gnn_in['W'], 'L1_gnn_a': _L1_gnn_in['a']}

def reference(x, adj, L0_gnn_attn_w, L0_gnn_attn_b, L0_gnn_W1, L0_gnn_b1, L0_gnn_W2, L0_gnn_b2, L0_gnn_g1, L0_gnn_beta1, L0_gnn_g2, L0_gnn_beta2, L1_gnn_W, L1_gnn_a):
    import jax
    import jax.numpy as jnp

    def _L0_gnn_ref(node_features, adjacency_matrix, attn_w, attn_b, W1, b1, W2, b2, g1, beta1, g2, beta2):
        import jax, jax.numpy as jnp
        import numpy as np
        L = 3
        D = 256
        B, N = (8, 512)
        EPS = 1e-05

        def layernorm(x, gamma, beta):
            mu = jnp.mean(x, axis=-1, keepdims=True)
            var = jnp.var(x, axis=-1, keepdims=True)
            return (x - mu) * jax.lax.rsqrt(var + EPS) * gamma + beta
        n = adjacency_matrix.shape[-1]
        mask = adjacency_matrix.astype(jnp.float32) + jnp.eye(n, dtype=jnp.float32) > 0
        x = node_features
        d = x.shape[-1]
        for l in range(attn_w.shape[0]):
            si = x @ attn_w[l, :d]
            sj = x @ attn_w[l, d:]
            scores = si[:, :, None] + sj[:, None, :] + attn_b[l]
            scores = jnp.where(scores >= 0, scores, 0.2 * scores)
            scores = jnp.where(mask, scores, -jnp.inf)
            attn = jax.nn.softmax(scores, axis=-1)
            agg = jnp.einsum('bij,bjd->bid', attn, x)
            h = layernorm(x + agg, g1[l], beta1[l])
            ff = jax.nn.gelu(h @ W1[l] + b1[l], approximate=False) @ W2[l] + b2[l]
            x = layernorm(h + ff, g2[l], beta2[l])
        return x

    def _L1_gnn_ref(h, W, a, adj):
        import jax, jax.numpy as jnp
        import numpy as np
        ALPHA = 0.2

        def _leaky(x):
            return jnp.where(x >= 0, x, ALPHA * x)
        F_out = W.shape[1]
        Wh = jnp.matmul(h, W)
        Wh_sg = jax.lax.stop_gradient(Wh)
        a1 = a[:F_out, 0]
        a2 = a[F_out:, 0]
        s_i = Wh_sg @ a1
        s_j = Wh_sg @ a2
        e = _leaky(s_i[:, :, None] + s_j[:, None, :])
        e = jnp.where(adj > 0, e, jnp.float32(-9000000000000000.0))
        attention = jax.nn.softmax(e, axis=1)
        h_prime = jnp.einsum('bij,bjf->bif', attention, Wh)
        return _leaky(h_prime)
    h = jnp.maximum(_layernorm(x, axis=-1), 0.0)
    x = x + _L0_gnn_ref(h, adj, L0_gnn_attn_w, L0_gnn_attn_b, L0_gnn_W1, L0_gnn_b1, L0_gnn_W2, L0_gnn_b2, L0_gnn_g1, L0_gnn_beta1, L0_gnn_g2, L0_gnn_beta2)
    h = jnp.maximum(_layernorm(x, axis=-1), 0.0)
    x = x + _L1_gnn_ref(h, L1_gnn_W, L1_gnn_a, adj)
    return x

_drawn_inputs = setup_inputs


def setup_inputs(seed=0):
    import zlib

    import numpy as np

    out = dict(_drawn_inputs(seed))
    spreads = {'L0_gnn_b1': (0.0, 0.1),
     'L0_gnn_b2': (0.0, 0.1),
     'L0_gnn_g1': (1.0, 0.2),
     'L0_gnn_beta1': (0.0, 0.1),
     'L0_gnn_g2': (1.0, 0.2),
     'L0_gnn_beta2': (0.0, 0.1)}
    factors = {'L0_gnn_attn_b': 64.0}
    for name, (base, spread) in spreads.items():
        noise = np.random.default_rng([zlib.crc32(name.encode()), seed]).standard_normal(out[name].shape)
        drawn = base * np.exp(spread * noise) if base else spread * noise
        out[name] = jnp.asarray(drawn.astype(out[name].dtype))
    for name, factor in factors.items():
        out[name] = (out[name] * factor).astype(out[name].dtype)
    return out
```

```python
from contextlib import ExitStack

import concourse.bass as bass
from concourse import mybir

F32 = mybir.dt.float32
F32R = mybir.dt.float32r
BF16 = mybir.dt.bfloat16
I32 = mybir.dt.int32
ALU = mybir.AluOpType
ACT = mybir.ActivationFunctionType

P = 128
EPS = 1e-5
SLOPE = 0.2
MASKED = -1e30



class Counted:

    def __init__(self, sem, per, unit):
        self.sem, self.per, self.unit = sem, per, unit

    def at(self, step, k=None):
        return step * (self.per * self.unit) + (self.per if k is None else k) * self.unit


def begun(value):
    return not isinstance(value, int) or value > 0


def gnn_program(nc, x, adj, attn_w, attn_b, W1, b1, W2, b2, g1, beta1, g2, beta2, Wl, al, out):
    B, N, D = x.shape
    LAYERS, _, F = W1.shape
    NC = N // P
    KC = D // P
    FC = F // P
    STEPS = 2 * LAYERS
    PAIRS = B // 2
    RING = 3
    LAG = 2
    LAST = LAYERS - 1

    with ExitStack() as ctx:
        def sb(name, shape, dt):
            return ctx.enter_context(nc.sbuf_tensor(name, shape, dt))

        def sem(name, per=1, unit=1):
            return Counted(ctx.enter_context(nc.semaphore(name)), per, unit)

        w1_hi = sb("w1_hi", [P, LAYERS, KC, F], F32R)
        w1_lo = sb("w1_lo", [P, LAYERS, KC, F], F32R)
        w2_hi = sb("w2_hi", [P, LAYERS, FC, D], F32R)
        w2_lo = sb("w2_lo", [P, LAYERS, FC, D], F32R)
        w_last = sb("w_last", [P, KC, D + 2], F32)
        VECS = LAYERS * (FC + 2 * KC)
        vec_col = sb("vec_col", [P, VECS], F32)
        b1_col = vec_col[:, 0:LAYERS * FC].rearrange("p (l c) -> p l c", l=LAYERS)
        g1_col = vec_col[:, LAYERS * FC:LAYERS * (FC + KC)].rearrange("p (l c) -> p l c", l=LAYERS)
        beta1_col = vec_col[:, LAYERS * (FC + KC):VECS].rearrange("p (l c) -> p l c", l=LAYERS)
        attn_row = sb("attn_row", [P, LAYERS, 2, D], F32)
        g2_row = sb("g2_row", [P, LAYERS, D], F32)
        beta2_row = sb("beta2_row", [P, LAYERS, D], F32)
        bias_col = sb("bias_col", [P, 2, LAYERS], F32)
        b2_parts = sb("b2_parts", [2, LAYERS, D], F32R)
        minus_row = sb("minus_row", [2, 1], F32)
        ones_r = sb("ones_r", [2, P], F32R)
        ident = sb("ident", [P, P], F32)
        ident_r = sb("ident_r", [P, P], F32R)
        ident_b = sb("ident_b", [P, P], BF16)
        minus_half = sb("minus_half", [P, NC], F32)
        x_nat = sb("x_nat", [P, 2, NC, D + 1], F32)
        h_hi = sb("h_hi", [P, KC, N], F32R)
        h_lo = sb("h_lo", [P, KC, N], F32R)
        mask_nat = sb("mask_nat", [P, 2, NC, N], BF16)
        mask_t = sb("mask_t", [P, 2, NC, N], BF16)
        diag_t = sb("diag_t", [P, 2, NC, P], BF16)
        diag_nat = sb("diag_nat", [P, NC, P], BF16)
        adj_in = sb("adj_in", [P, 2, N], I32)
        adj_self = sb("adj_self", [P, P], F32)
        x_res = sb("x_res", [P, 2, NC, D], F32)
        mask_g = sb("mask_g", [P, NC, N], BF16)
        probs = sb("probs", [P, NC, N], F32)
        g_full = sb("g_full", [P, 2, N], F32)
        gelu_hi = sb("gelu_hi", [P, RING, N], F32R)
        gelu_lo = sb("gelu_lo", [P, RING, N], F32R)
        normed = sb("normed", [P, NC, D], F32)
        wh = sb("wh", [P, NC, D], F32)
        low_sb = sb("low_sb", [P, N], F32)
        h_last = sb("h_last", [P, KC, N], F32)
        stats = sb("stats", [P, NC, 6], F32)
        mean_sum = sb("mean_sum", [P, NC], F32)
        mean_gap = sb("mean_gap", [P, NC], F32)
        squares = sb("squares", [P, NC], F32)
        gap_sq = sb("gap_sq", [P, NC], F32)
        mean = sb("mean", [P, NC], F32)
        var_eps = sb("var_eps", [P, NC], F32)
        rstd = sb("rstd", [P, NC], F32)
        s_i = sb("s_i", [P, NC], F32)
        s_j = sb("s_j", [P, NC], F32)
        s_j8 = sb("s_j8", [P, NC], F32)
        s_j2 = sb("s_j2", [P, NC], F32)
        s_max = sb("s_max", [P, NC], F32)
        sg_i = sb("sg_i", [P, NC], F32)
        sg_j = sb("sg_j", [P, NC], F32)
        sg_j8 = sb("sg_j8", [P, NC], F32)
        sg_low = sb("sg_low", [P, NC], F32)
        o_tmp = sb("o_tmp", [P, 2, D], F32)
        top = sb("top", [P, NC], F32)
        high = sb("high", [P, NC], F32)
        low = sb("low", [P, NC], F32)
        r_sum = sb("r_sum", [P, NC], F32)
        col_max = sb("col_max", [P, NC], F32)
        col_neg = sb("col_neg", [P, NC], F32)
        col_sum = sb("col_sum", [P, NC], F32)
        col_r = sb("col_r", [P, NC], F32)

        h_full = probs[:, 0:KC, :]
        junk = h_last[:, :, :].rearrange("p k n -> p (k n)").bitcast(BF16)
        a_row = normed[:, 0:2, :]
        b2_two = wh[0:2, 0:LAYERS, :]
        ones_f = wh[0:2, LAYERS, 0:P]
        b2_round = h_last[0:2, :, :].rearrange("p k n -> p (k n)")[:, 0:LAYERS * D].bitcast(F32R).rearrange(
            "p (l d) -> p l d", l=LAYERS)

        def bank(name):
            return ctx.enter_context(nc.psum_tensor(name, [P, 512], F32))

        ps_u = [bank("ps_u0"), bank("ps_u1")]
        ps_d = [bank("ps_d0"), bank("ps_d1")]
        ps_a = [bank("ps_a0"), bank("ps_a1")]
        ps_t = [bank("ps_t0"), bank("ps_t1")]

        loaded = sem("loaded", 1, 16)
        weights_in = [sem(f"weights_in{i}", 1, 16) for i in range(2)]
        consts = sem("consts")
        split_w = sem("split_w")
        vec_tr = sem("vec_tr")
        vec_ready = sem("vec_ready")
        setup_v = sem("setup_v")
        x_loaded = [sem(f"x_loaded{side}", 1, 16) for side in range(2)]
        adj_loaded = [sem(f"adj_loaded{i}", NC // 2, 16) for i in range(2)]
        ln0_chain = sem("ln0_chain", 4)
        ln0_rstd = sem("ln0_rstd")
        ln0_apply = sem("ln0_apply")
        x0_ready = sem("x0_ready")
        self_added = sem("self_added", NC)
        nat_ready = sem("nat_ready", NC)
        mask_pe = sem("mask_pe", NC + 1)
        mask_ready = sem("mask_ready", NC + 1)
        s_ready = sem("s_ready")
        sj_bc = sem("sj_bc")
        max_ready = sem("max_ready")
        row_chain = sem("row_chain", 3)
        rows_bc = sem("rows_bc", 2)
        low_ready = sem("low_ready")
        q_ready = sem("q_ready", NC)
        q_masked = sem("q_masked", NC)
        p_ready = sem("p_ready", NC)
        agg_done = sem("agg_done", NC)
        rsum_ready = sem("rsum_ready", NC)
        y_ready = sem("y_ready", NC)
        ln1_chain = sem("ln1_chain", 4)
        ln1_rstd = sem("ln1_rstd")
        ln1_apply = sem("ln1_apply")
        h_tr = sem("h_tr", KC)
        h_act = sem("h_act", KC)
        h_ready = sem("h_ready", KC)
        u_done = sem("u_done", FC)
        gelu_done = sem("gelu_done", FC)
        lo_done = [sem(f"lo_done{i}", FC // 2) for i in range(2)]
        d_used = sem("d_used", FC - 1)
        d_done = sem("d_done", 2)
        ln2_chain = sem("ln2_chain", 4)
        ln2_rstd = sem("ln2_rstd")
        ln2_apply = sem("ln2_apply")
        x_scaled = sem("x_scaled")
        x_ready = sem("x_ready")
        res_loaded = [sem(f"res_loaded{side}", 1, 16) for side in range(2)]
        res_beta = sem("res_beta")
        lng_chain = sem("lng_chain", 4)
        lng_rstd = sem("lng_rstd")
        lng_apply = sem("lng_apply")
        g_tr = sem("g_tr", KC)
        g_act = sem("g_act", KC)
        wh_done = sem("wh_done", NC)
        wh_copy = sem("wh_copy", NC)
        sg_copy = sem("sg_copy", NC)
        sg_rows = sem("sg_rows")
        mask_g_ready = sem("mask_g_ready", 2)
        g_rows = sem("g_rows", 2)
        g_low = sem("g_low")
        g_q = sem("g_q", NC)
        g_max = sem("g_max", NC)
        g_neg = sem("g_neg", NC)
        g_exp = sem("g_exp", NC)
        g_r = sem("g_r")
        wh_scaled = sem("wh_scaled")
        o_done = sem("o_done", NC)
        o_low = sem("o_low", NC)
        o_leaky = sem("o_leaky", NC)
        o_ready = sem("o_ready", NC)
        stored = [sem(f"stored{side}", NC, 16) for side in range(2)]

        block = ctx.enter_context(nc.Block())

        stage = [probs[:, :, :].rearrange("p c n -> p (c n)"), x_res[:, :, :, :].rearrange("p s c d -> p (s c d)")]
        weight_loads = []
        for l in range(LAYERS):
            weight_loads.append((W1[l].rearrange("(k p) f -> p k f", p=P), w1_hi[:, l], w1_lo[:, l], KC, F))
            weight_loads.append((W2[l].rearrange("(k p) f -> p k f", p=P), w2_hi[:, l], w2_lo[:, l], FC, D))
        SETUP = 4 + 4 * (LAYERS - 1) + 2 * KC
        SMALL = 10

        def staged(i):
            _, _, _, k, n = weight_loads[i]
            return stage[i % 2][:, 0:k * n].rearrange("p (k n) -> p k n", k=k)

        def each_pair(engine, body):
            body(0, True, PAIRS == 1)
            if PAIRS > 2:
                with engine.Fori(1, PAIRS - 1) as pair:
                    body(pair, False, False)
            if PAIRS > 1:
                body(PAIRS - 1, False, True)

        def slots(pair, first, last):
            for layer in range(LAYERS):
                for side in range(2):
                    n = pair * STEPS + 2 * layer + side
                    final = None
                    if side == 1 and layer == LAST:
                        final = pair * 2
                    if side == 0 and layer == 0 and not first:
                        final = pair * 2 - 1
                    prepare = pair * 2 + 2 + side if layer == LAST and not last else None
                    attend = not (side == 1 and layer == LAST and last)
                    yield n, side, layer, final, prepare, attend, (layer + side) % LAYERS

        @block.sync
        def _(sp):
            small = [
                (low_sb[0:LAYERS * FC, 0:P], b1.rearrange("l (c p) -> (l c) p", p=P)),
                (low_sb[LAYERS * FC:LAYERS * (FC + KC), 0:P], g1.rearrange("l (c p) -> (l c) p", p=P)),
                (low_sb[LAYERS * (FC + KC):VECS, 0:P], beta1.rearrange("l (c p) -> (l c) p", p=P)),
                (attn_row[:, :, :, :], attn_w.rearrange("(o l) (t d) -> o l t d", o=1, t=2).broadcast_to([P, LAYERS, 2, D])),
                (w_last[:, :, 0:D], Wl.rearrange("(k p) f -> p k f", p=P)),
                (a_row, al.rearrange("(t d) o -> o t d", t=2).broadcast_to([P, 2, D])),
                (g2_row[:, :, :], g2.rearrange("(o l) d -> o l d", o=1).broadcast_to([P, LAYERS, D])),
                (beta2_row[:, :, :], beta2.rearrange("(o l) d -> o l d", o=1).broadcast_to([P, LAYERS, D])),
                (b2_two, b2.rearrange("(o l) d -> o l d", o=1).broadcast_to([2, LAYERS, D])),
                (bias_col[:, 0, :], attn_b.rearrange("(o l) -> o l", o=1).broadcast_to([P, LAYERS])),
            ]
            assert len(small) == SMALL

            def load_input(g, side, step_before):
                if step_before is not None:
                    sp.wait_ge(y_ready.sem, y_ready.at(step_before))
                sp.dma_start(x_nat[:, side, :, 0:D], x[g].rearrange("(c p) d -> p c d", p=P)).then_inc(x_loaded[side].sem, 16)
                for c in range(NC):
                    if begun(self_added.at(g, c - 1)):
                        sp.wait_ge(self_added.sem, self_added.at(g, c - 1))
                    sp.dma_start(adj_in[:, c % 2, :], adj[g][c * P:(c + 1) * P, :]).then_inc(adj_loaded[c % 2].sem, 16)

            def load_residual(pair, side):
                g = pair * 2 + side
                if begun(stored[side].at(pair - 1)):
                    sp.wait_ge(stored[side].sem, stored[side].at(pair - 1))
                sp.dma_start(x_res[:, side, :, :], x[g].rearrange("(c p) d -> p c d", p=P)).then_inc(res_loaded[side].sem, 16)

            def store(g, side):
                for c in range(NC):
                    sp.wait_ge(o_ready.sem, o_ready.at(g, c + 1))
                    sp.dma_start(out[g][c * P:(c + 1) * P, :], x_res[:, side, c, :]).then_inc(stored[side].sem, 16)

            for dst, src in small:
                sp.dma_start(dst, src).then_inc(loaded.sem, 16)
            sp.wait_ge(consts.sem, consts.at(0))
            load_input(0, 0, None)
            for i, (src, _, _, _, _) in enumerate(weight_loads):
                if begun(split_w.at(2 * i - 3)):
                    sp.wait_ge(split_w.sem, split_w.at(2 * i - 3))
                sp.dma_start(staged(i), src).then_inc(weights_in[i % 2].sem, 16)
            load_input(1, 1, None)

            def pair_body(pair, first, last):
                for n, side, layer, final, prepare, attend, _ in slots(pair, first, last):
                    if layer == 0 and not first:
                        store(pair * 2 - 2 + side, side)
                    if layer == LAST:
                        load_residual(pair, side)
                    if prepare is not None:
                        load_input(prepare, side, n)

            each_pair(sp, pair_body)
            for side in range(2):
                store(B - 2 + side, side)
            for side in range(2):
                sp.wait_ge(stored[side].sem, stored[side].at(PAIRS - 1))

        @block.tensor
        def _(pe):
            def columns_to_rows(bank_n, col):
                for c in range(NC):
                    last = pe.transpose(ps_t[bank_n][:, c * P:(c + 1) * P], col[:, c:c + 1].broadcast_to([P, P]),
                                        ident[:, :])
                return last

            def mask_transposes(g, side, free0, free1):
                pe.wait_ge(*free0)
                pe.wait_ge(*free1)
                for c in range(NC + 1):
                    view = ps_t[c % 2][:, :].bitcast(BF16)
                    if c >= 2:
                        pe.wait_ge(mask_ready.sem, mask_ready.at(g, c - 1))
                    if c < NC:
                        pe.wait_ge(nat_ready.sem, nat_ready.at(g, c + 1))
                    for j in range(NC):
                        block = mask_nat[:, side, c, j * P:(j + 1) * P] if c < NC else diag_nat[:, j, :]
                        last = pe.transpose(view[:, j * P:(j + 1) * P], block, ident_b[:, :])
                    last.then_inc(mask_pe.sem, 1)

            def scores_row(n, free0):
                pe.wait_ge(s_ready.sem, s_ready.at(n))
                pe.wait_ge(*free0)
                columns_to_rows(0, s_j).then_inc(sj_bc.sem, 1)

            def bound_rows(n, free1):
                pe.wait_ge(row_chain.sem, row_chain.at(n))
                pe.wait_ge(*free1)
                columns_to_rows(1, high).then_inc(rows_bc.sem, 1)
                pe.wait_ge(max_ready.sem, max_ready.at(n))
                columns_to_rows(0, low).then_inc(rows_bc.sem, 1)

            def attend_out(n, side, layer, g, read):
                if layer == 0:
                    pe.wait_ge(x0_ready.sem, x0_ready.at(g))
                else:
                    pe.wait_ge(x_ready.sem, x_ready.at(n - 2))
                for c in range(NC):
                    if c >= 2:
                        pe.wait_ge(y_ready.sem, y_ready.at(n, c - 1))
                    elif read is not None:
                        pe.wait_ge(read[0].sem, read[0].at(read[1], NC - 1 + c))
                    for j in range(NC):
                        if c == 0:
                            pe.wait_ge(p_ready.sem, p_ready.at(n, j + 1))
                        last = pe.matmul(ps_a[c % 2][:, 0:D + 1], probs[:, j, c * P:(c + 1) * P], x_nat[:, side, j, :],
                                         start=(j == 0), stop=(j == NC - 1))
                    last.then_inc(agg_done.sem, 1)

            def turn_tokens(applied, turned, step, free0, free1):
                pe.wait_ge(applied.sem, applied.at(step))
                for k in range(KC):
                    pe.wait_ge(*(free0, free1)[k])
                    for c in range(NC):
                        last = pe.transpose(ps_t[k][:, c * P:(c + 1) * P], normed[:, c, k * P:(k + 1) * P], ident[:, :])
                    last.then_inc(turned.sem, 1)

            def up(n, side, layer, f):
                if f == 0:
                    pe.wait_ge(h_ready.sem, h_ready.at(n))
                if begun(gelu_done.at(n, f - 1)):
                    pe.wait_ge(gelu_done.sem, gelu_done.at(n, f - 1))
                lhs = slice(f * P, (f + 1) * P)
                terms = [(w, h, k) for k in range(KC) for w, h in ((w1_hi, h_hi), (w1_hi, h_lo), (w1_lo, h_hi))]
                for i, (w, h, k) in enumerate(terms):
                    last = pe.matmul(ps_u[f % 2][:, :], w[:, layer, k, lhs], h[:, k, :],
                                     start=(i == 0), stop=(i == len(terms) - 1))
                last.then_inc(u_done.sem, 1)

            def residual(n, side, layer):
                if begun(ln2_apply.at(n - 1)):
                    pe.wait_ge(ln2_apply.sem, ln2_apply.at(n - 1))
                for c in range(NC):
                    cols = (c % 2) * D
                    dst = ps_d[c // 2]
                    for k in range(KC):
                        for i, h in enumerate((h_hi, h_lo)):
                            pe.matmul(dst[:, cols + k * P:cols + (k + 1) * P], h[:, k, c * P:(c + 1) * P],
                                      ident_r[:, :], start=(c % 2 == 0 and k == 0 and i == 0), stop=False,
                                      skip_group_check=True)
                    pe.matmul(dst[:, cols:cols + D], ones_r[:, :], b2_parts[:, layer, :], start=False, stop=False,
                              skip_group_check=True)

            def down(n, side, layer, f):
                if f == 0:
                    residual(n, side, layer)
                pe.wait_ge(lo_done[f % 2].sem, lo_done[f % 2].at(n, f // 2 + 1))
                r = f % RING
                for c in range(NC):
                    cols = (c % 2) * D
                    tok = slice(c * P, (c + 1) * P)
                    for i, (h, w) in enumerate(((gelu_hi, w2_hi), (gelu_hi, w2_lo), (gelu_lo, w2_hi))):
                        last = pe.matmul(ps_d[c // 2][:, cols:cols + D], h[:, r, tok], w[:, layer, f, :],
                                         start=False, stop=(f == FC - 1 and i == 2), skip_group_check=True)
                    if f == FC - 1 and c % 2 == 1:
                        last.then_inc(d_done.sem, 1)
                    if f < FC - 1 and c == NC - 1:
                        last.then_inc(d_used.sem, 1)

            def project(g, read):
                pe.wait_ge(g_act.sem, g_act.at(g))
                for c in range(NC):
                    if c >= 2:
                        pe.wait_ge(sg_copy.sem, sg_copy.at(g, c - 1))
                    else:
                        pe.wait_ge(read[0].sem, read[0].at(read[1], NC - 1 + c))
                    for k in range(KC):
                        last = pe.matmul(ps_a[c % 2][:, 0:D + 2], h_last[:, k, c * P:(c + 1) * P], w_last[:, k, :],
                                         start=(k == 0), stop=(k == KC - 1))
                    last.then_inc(wh_done.sem, 1)

            def final_rows(g, free0, free1):
                pe.wait_ge(sg_rows.sem, sg_rows.at(g))
                pe.wait_ge(*free1)
                columns_to_rows(1, sg_i).then_inc(g_rows.sem, 1)
                pe.wait_ge(*free0)
                columns_to_rows(0, sg_low).then_inc(g_rows.sem, 1)

            def final_out(g, read):
                pe.wait_ge(wh_scaled.sem, wh_scaled.at(g))
                for c in range(NC):
                    if c >= 2:
                        pe.wait_ge(o_leaky.sem, o_leaky.at(g, c - 1))
                    else:
                        pe.wait_ge(read[0].sem, read[0].at(read[1], NC - 1 + c))
                    for j in range(NC):
                        last = pe.matmul(ps_a[c % 2][:, 0:D], probs[:, j, c * P:(c + 1) * P], wh[:, j, :],
                                         start=(j == 0), stop=(j == NC - 1))
                    last.then_inc(o_done.sem, 1)

            pe.wait_ge(consts.sem, consts.at(2))
            pe.wait_ge(loaded.sem, loaded.at(SMALL - 1))
            pe.transpose(ps_t[0][:, 0:VECS], low_sb[0:VECS, 0:P], ident[0:VECS, 0:VECS]).then_inc(vec_tr.sem, 1)
            copied = (vec_ready.sem, vec_ready.at(0))
            mask_transposes(0, 0, copied, copied)
            scores_row(0, (mask_ready.sem, mask_ready.at(0, NC + 1)))
            bound_rows(0, (mask_ready.sem, mask_ready.at(0, NC)))
            attend_out(0, 0, 0, 0, None)
            turn_tokens(ln1_apply, h_tr, 0, (low_ready.sem, low_ready.at(0)), (q_ready.sem, q_ready.at(0)))
            mask_transposes(1, 1, (h_act.sem, h_act.at(0, 1)), (h_act.sem, h_act.at(0, 2)))
            pe.wait_ge(split_w.sem, split_w.at(2 * len(weight_loads) - 1))
            pe.wait_ge(setup_v.sem, setup_v.at(SETUP - 1))

            def pair_body(pair, first, last):
                for n, side, layer, final, prepare, attend, layer_a in slots(pair, first, last):
                    other = 1 - side
                    graph_a = pair * 2 + 1 if side == 0 else pair * 2 + 2
                    late = pair * 2 - 2 + side if layer == 0 and not first else None
                    if layer == 0 and not first:
                        free0 = (g_low.sem, g_low.at(late))
                        free1 = (g_q.sem, g_q.at(late))
                    elif first and n == 0:
                        free0 = (mask_ready.sem, mask_ready.at(1, NC + 1))
                        free1 = (mask_ready.sem, mask_ready.at(1, NC))
                    else:
                        free0 = (h_act.sem, h_act.at(n, 1))
                        free1 = (h_act.sem, h_act.at(n, 2))
                    read = (y_ready, n)
                    for f in range(FC + LAG):
                        if f < FC:
                            up(n, side, layer, f)
                        if f >= LAG:
                            down(n, side, layer, f - LAG)
                        if f == 0 and side == 0 and late is not None:
                            mask_transposes(pair * 2 + 1, 1, free0, free1)
                            free0 = (mask_ready.sem, mask_ready.at(pair * 2 + 1, NC + 1))
                            free1 = (mask_ready.sem, mask_ready.at(pair * 2 + 1, NC))
                        if f == 1 and late is not None:
                            final_out(late, read)
                            read = (o_leaky, late)
                        if attend and f == (2 if final is None else 1):
                            scores_row(n + 1, free0)
                        if attend and f == (3 if final is None else 2):
                            bound_rows(n + 1, free1)
                            free0 = (low_ready.sem, low_ready.at(n + 1))
                            free1 = (q_ready.sem, q_ready.at(n + 1))
                        if final is not None and f == 4:
                            turn_tokens(lng_apply, g_tr, final, free0, free1)
                            free0 = (g_act.sem, g_act.at(final, 1))
                            free1 = (g_act.sem, g_act.at(final, 2))
                        if final is not None and f == 5:
                            project(final, read)
                            read = (sg_copy, final)
                        if attend and f == (5 if final is None else 6):
                            attend_out(n + 1, other, layer_a, graph_a, read)
                        if prepare is not None and side == 0 and f == 7:
                            mask_transposes(prepare, 0, free0, free1)
                            free0 = (mask_ready.sem, mask_ready.at(prepare, NC + 1))
                            free1 = (mask_ready.sem, mask_ready.at(prepare, NC))
                        if attend and f == (8 if final is None else 9):
                            turn_tokens(ln1_apply, h_tr, n + 1, free0, free1)
                            free0 = (h_act.sem, h_act.at(n + 1, 1))
                            free1 = (h_act.sem, h_act.at(n + 1, 2))
                        if final is not None and f == 9:
                            final_rows(final, free0, free1)

            each_pair(pe, pair_body)
            final_out(B - 2, (sg_copy, B - 2))
            turn_tokens(lng_apply, g_tr, B - 1, (g_low.sem, g_low.at(B - 2)), (g_q.sem, g_q.at(B - 2)))
            project(B - 1, (o_leaky, B - 2))
            final_rows(B - 1, (g_act.sem, g_act.at(B - 1, 1)), (g_act.sem, g_act.at(B - 1, 2)))
            final_out(B - 1, (sg_copy, B - 1))

        @block.scalar
        def _(act):
            def mask_copies(g, side):
                if begun(mask_g_ready.at(g - 2)):
                    act.wait_ge(mask_g_ready.sem, mask_g_ready.at(g - 2))
                for c in range(NC):
                    act.wait_ge(mask_pe.sem, mask_pe.at(g, c + 1))
                    src = ps_t[c % 2][:, :].bitcast(BF16)[:, 0:N].rearrange("p (j i) -> p j i", i=P)
                    act.activation(mask_t[:, side, :, c * P:(c + 1) * P], src, ACT.Copy).then_inc(mask_ready.sem, 1)
                act.wait_ge(mask_pe.sem, mask_pe.at(g, NC + 1))
                src = ps_t[NC % 2][:, :].bitcast(BF16)[:, 0:N].rearrange("p (j i) -> p j i", i=P)
                act.activation(diag_t[:, side, :, :], src, ACT.Copy).then_inc(mask_ready.sem, 1)

            def low_row(n):
                act.wait_ge(rows_bc.sem, rows_bc.at(n, 2))
                act.activation(low_sb[:, :], ps_t[0][:, :], ACT.Copy).then_inc(low_ready.sem, 1)

            def exps(n):
                for j in range(NC):
                    act.wait_ge(q_masked.sem, q_masked.at(n, j + 1))
                    act.activation(probs[:, j, :], probs[:, j, :], ACT.Exp, bias=s_j2[:, j:j + 1]).then_inc(p_ready.sem, 1)

            def h_split(n, side, layer):
                for k in range(KC):
                    act.wait_ge(h_tr.sem, h_tr.at(n, k + 1))
                    act.activation(h_full[:, k, :], ps_t[k][:, :], ACT.Identity, bias=beta1_col[:, layer, k:k + 1],
                                   scale=g1_col[:, layer, k:k + 1])
                    act.activation(h_hi[:, k, :], ps_t[k][:, :], ACT.Identity,
                                   bias=beta1_col[:, layer, k:k + 1], scale=g1_col[:, layer, k:k + 1]).then_inc(h_act.sem, 1)

            def gelu(n, layer, f):
                act.wait_ge(u_done.sem, u_done.at(n, f + 1))
                if begun(lo_done[f % 2].at(n, f // 2)):
                    act.wait_ge(lo_done[f % 2].sem, lo_done[f % 2].at(n, f // 2))
                act.activation(g_full[:, f % 2, :], ps_u[f % 2][:, :], ACT.Gelu, bias=b1_col[:, layer, f:f + 1])
                if f >= RING:
                    act.wait_ge(d_used.sem, d_used.at(n, f - RING + 1))
                act.activation(gelu_hi[:, f % RING, :], ps_u[f % 2][:, :], ACT.Gelu,
                               bias=b1_col[:, layer, f:f + 1]).then_inc(gelu_done.sem, 1)

            def final_h(g):
                for k in range(KC):
                    act.wait_ge(g_tr.sem, g_tr.at(g, k + 1))
                    act.activation(h_last[:, k, :], ps_t[k][:, :], ACT.Relu).then_inc(g_act.sem, 1)

            def final_wh(g):
                for c in range(NC):
                    act.wait_ge(wh_done.sem, wh_done.at(g, c + 1))
                    act.activation(wh[:, c, :], ps_a[c % 2][:, 0:D], ACT.Copy).then_inc(wh_copy.sem, 1)

            def final_low(g):
                act.wait_ge(g_rows.sem, g_rows.at(g, 2))
                act.activation(low_sb[:, :], ps_t[0][:, :], ACT.Copy).then_inc(g_low.sem, 1)

            def final_exps(g):
                for j in range(NC):
                    act.wait_ge(g_neg.sem, g_neg.at(g, j + 1))
                    act.activation(probs[:, j, :], probs[:, j, :], ACT.Exp, bias=col_neg[:, j:j + 1],
                                   accum_out=col_sum[:, j:j + 1]).then_inc(g_exp.sem, 1)

            def final_leaky(g):
                for c in range(NC):
                    act.wait_ge(o_done.sem, o_done.at(g, c + 1))
                    if c >= 2:
                        act.wait_ge(o_ready.sem, o_ready.at(g, c - 1))
                    act.activation(o_tmp[:, c % 2, :], ps_a[c % 2][:, 0:D], ACT.Copy, scale=SLOPE).then_inc(o_low.sem, 1)

            act.wait_ge(vec_tr.sem, vec_tr.at(0))
            act.activation(vec_col[:, :], ps_t[0][:, 0:VECS], ACT.Copy).then_inc(vec_ready.sem, 1)
            act.wait_ge(vec_ready.sem, vec_ready.at(0))
            mask_copies(0, 0)
            low_row(0)
            exps(0)
            h_split(0, 0, 0)
            mask_copies(1, 1)

            def pair_body(pair, first, last):
                for n, side, layer, final, prepare, attend, layer_a in slots(pair, first, last):
                    other = 1 - side
                    for f in range(FC + LAG):
                        if f < FC:
                            gelu(n, layer, f)
                        if f == 0 and layer == 0 and side == 0 and not first:
                            mask_copies(pair * 2 + 1, 1)
                        if f == 1 and layer == 0 and not first:
                            final_leaky(pair * 2 - 2 + side)
                        if final is None:
                            if attend and f == 3:
                                low_row(n + 1)
                            if attend and f == 4:
                                exps(n + 1)
                            if prepare is not None and f == 7:
                                mask_copies(prepare, 0)
                            if attend and f == 8:
                                h_split(n + 1, other, layer_a)
                        else:
                            if attend and f == 2:
                                low_row(n + 1)
                            if attend and f == 4:
                                exps(n + 1)
                            if f == 4:
                                final_h(final)
                            if f == 5:
                                final_wh(final)
                            if f == 9:
                                if attend:
                                    h_split(n + 1, other, layer_a)
                                final_low(final)
                                final_exps(final)

            each_pair(act, pair_body)
            final_leaky(B - 2)
            final_h(B - 1)
            final_wh(B - 1)
            final_low(B - 1)
            final_exps(B - 1)
            final_leaky(B - 1)

        @block.vector
        def _(dve):
            def norm_stats(source, chain, idx):
                for c in range(NC):
                    last = dve.bn_stats(stats[:, c, :], source(c))
                last.then_inc(chain.sem, 1)
                dve.wait_ge(chain.sem, chain.at(idx, 1))
                dve.tensor_tensor(mean_sum[:, :], stats[:, :, 1], stats[:, :, 4], ALU.add)
                dve.tensor_tensor(mean_gap[:, :], stats[:, :, 1], stats[:, :, 4], ALU.subtract)
                dve.scalar_tensor_tensor(out=squares[:, :], in0=stats[:, :, 2], scalar=D * EPS,
                                         in1=stats[:, :, 5], op0=ALU.add, op1=ALU.add).then_inc(chain.sem, 1)
                dve.wait_ge(chain.sem, chain.at(idx, 2))
                dve.tensor_scalar(mean[:, :], mean_sum[:, :], 0.5, None, ALU.mult)
                dve.scalar_tensor_tensor(out=gap_sq[:, :], in0=mean_gap[:, :], scalar=0.25,
                                         in1=mean_gap[:, :], op0=ALU.mult, op1=ALU.mult).then_inc(chain.sem, 1)
                dve.wait_ge(chain.sem, chain.at(idx, 3))
                dve.scalar_tensor_tensor(out=var_eps[:, :], in0=squares[:, :], scalar=1.0 / D,
                                         in1=gap_sq[:, :], op0=ALU.mult, op1=ALU.add).then_inc(chain.sem, 1)

            def norm_apply(source, ready, idx, done):
                dve.wait_ge(ready.sem, ready.at(idx))
                for c in range(NC):
                    last = dve.tensor_scalar(normed[:, c, :], source(c), mean[:, c:c + 1], rstd[:, c:c + 1],
                                             ALU.subtract, ALU.mult)
                last.then_inc(done.sem, 1)
                dve.wait_ge(done.sem, done.at(idx))

            def prepare_masks(g, side):
                for c in range(NC):
                    blk = slice(c * P, (c + 1) * P)
                    dve.wait_ge(adj_loaded[c % 2].sem, adj_loaded[c % 2].at(g, c // 2 + 1))
                    dve.tensor_scalar(mask_nat[:, side, c, :], adj_in[:, c % 2, :], 0.0, MASKED, ALU.is_le, ALU.mult)
                    dve.tensor_scalar(diag_nat[:, c, :], adj_in[:, c % 2, blk], 0.0, MASKED, ALU.is_le, ALU.mult)
                    dve.tensor_tensor(adj_self[:, :], adj_in[:, c % 2, blk], ident[:, :], ALU.add).then_inc(self_added.sem, 1)
                    dve.wait_ge(self_added.sem, self_added.at(g, c + 1))
                    dve.tensor_scalar(mask_nat[:, side, c, blk], adj_self[:, :], 0.0, MASKED,
                                      ALU.is_le, ALU.mult).then_inc(nat_ready.sem, 1)
                    dve.wait_ge(nat_ready.sem, nat_ready.at(g, c + 1))

            def prepare_x(g, side, pair):
                dve.wait_ge(x_loaded[side].sem, x_loaded[side].at(pair))
                norm_stats(lambda c: x_nat[:, side, c, 0:D], ln0_chain, g)
                dve.wait_ge(ln0_rstd.sem, ln0_rstd.at(g))
                for c in range(NC):
                    last = dve.tensor_scalar(x_nat[:, side, c, 0:D], x_nat[:, side, c, 0:D], mean[:, c:c + 1],
                                             rstd[:, c:c + 1], ALU.subtract, ALU.mult)
                last.then_inc(ln0_apply.sem, 1)
                dve.wait_ge(ln0_apply.sem, ln0_apply.at(g))
                dve.tensor_scalar(x_nat[:, side, :, 0:D], x_nat[:, side, :, 0:D], 0.0, None, ALU.max).then_inc(x0_ready.sem, 1)
                dve.wait_ge(x0_ready.sem, x0_ready.at(g))

            def token_dots(source, row_i, row_j, init_i, init_j, to_i, to_j):
                for c in range(NC):
                    dve.tensor_tensor_reduce(junk[:, 2 * c * D:(2 * c + 1) * D], source(c), row_i, 1.0, init_i,
                                             ALU.mult, ALU.add, to_i[:, c:c + 1])
                    last = dve.tensor_tensor_reduce(junk[:, (2 * c + 1) * D:(2 * c + 2) * D], source(c), row_j, 1.0,
                                                    init_j, ALU.mult, ALU.add, to_j[:, c:c + 1])
                return last

            def neighbour_max(n, side):
                dve.wait_ge(sj_bc.sem, sj_bc.at(n))
                dve.tensor_scalar(s_j8[:, :], s_j[:, :], 1.0 - SLOPE, None, ALU.mult)
                dve.tensor_scalar(s_j2[:, :], s_j[:, :], SLOPE, None, ALU.mult)
                for c in range(NC):
                    last = dve.tensor_tensor_reduce(junk[:, c * N:(c + 1) * N], ps_t[0][:, :], mask_nat[:, side, c, :],
                                                    1.0, -3e38, ALU.add, ALU.max, s_max[:, c:c + 1])
                last.then_inc(max_ready.sem, 1)
                dve.wait_ge(max_ready.sem, max_ready.at(n))
                dve.tensor_tensor(high[:, :], s_i[:, :], s_max[:, :], ALU.add).then_inc(row_chain.sem, 1)
                dve.wait_ge(row_chain.sem, row_chain.at(n, 1))
                dve.scalar_tensor_tensor(out=top[:, :], in0=high[:, :], scalar=SLOPE, in1=high[:, :],
                                         op0=ALU.mult, op1=ALU.max).then_inc(row_chain.sem, 1)
                dve.wait_ge(row_chain.sem, row_chain.at(n, 2))
                dve.tensor_tensor(high[:, :], s_i[:, :], top[:, :], ALU.subtract)
                dve.scalar_tensor_tensor(out=low[:, :], in0=s_i[:, :], scalar=SLOPE, in1=top[:, :],
                                         op0=ALU.mult, op1=ALU.subtract).then_inc(row_chain.sem, 1)

            def bounded_scores(n, graph_before=None):
                dve.wait_ge(low_ready.sem, low_ready.at(n))
                dve.wait_ge(rows_bc.sem, rows_bc.at(n, 1))
                if begun(agg_done.at(n - 1)):
                    dve.wait_ge(agg_done.sem, agg_done.at(n - 1))
                if begun(h_ready.at(n - 1)):
                    dve.wait_ge(h_ready.sem, h_ready.at(n - 1))
                if graph_before is not None:
                    dve.wait_ge(o_done.sem, o_done.at(graph_before))
                for j in range(NC):
                    dve.scalar_tensor_tensor(out=probs[:, j, :], in0=ps_t[1][:, :], scalar=s_j8[:, j:j + 1],
                                             in1=low_sb[:, :], op0=ALU.add, op1=ALU.max).then_inc(q_ready.sem, 1)

            def attention_sum(n, side):
                for c in range(NC):
                    dve.wait_ge(agg_done.sem, agg_done.at(n, c + 1))
                    dve.reciprocal(r_sum[:, c:c + 1], ps_a[c % 2][:, D:D + 1]).then_inc(rsum_ready.sem, 1)
                    dve.wait_ge(rsum_ready.sem, rsum_ready.at(n, c + 1))
                    dve.scalar_tensor_tensor(out=normed[:, c, :], in0=ps_a[c % 2][:, 0:D],
                                             scalar=r_sum[:, c:c + 1], in1=x_nat[:, side, c, 0:D],
                                             op0=ALU.mult, op1=ALU.add).then_inc(y_ready.sem, 1)
                dve.wait_ge(y_ready.sem, y_ready.at(n))
                norm_stats(lambda c: normed[:, c, :], ln1_chain, n)

            def attention_norm(n):
                norm_apply(lambda c: normed[:, c, :], ln1_rstd, n, ln1_apply)

            def h_rest(n, side):
                for k in range(KC):
                    dve.wait_ge(h_act.sem, h_act.at(n, k + 1))
                    dve.tensor_tensor(h_lo[:, k, :], h_full[:, k, :],
                                      h_hi[:, k, :].bitcast(F32), ALU.subtract).then_inc(h_ready.sem, 1)

            def gelu_rest(n, f):
                dve.wait_ge(gelu_done.sem, gelu_done.at(n, f + 1))
                dve.tensor_tensor(gelu_lo[:, f % RING, :], g_full[:, 1, :],
                                  gelu_hi[:, f % RING, :].bitcast(F32), ALU.subtract).then_inc(lo_done[1].sem, 1)

            def ff_norm(n):
                def source(c):
                    return ps_d[c // 2][:, (c % 2) * D:(c % 2 + 1) * D]
                dve.wait_ge(d_done.sem, d_done.at(n))
                norm_stats(source, ln2_chain, n)
                norm_apply(source, ln2_rstd, n, ln2_apply)

            def layer_scores(n, layer, side):
                def source(c):
                    return x_nat[:, side, c, 0:D] if layer == 0 else normed[:, c, :]
                token_dots(source, attn_row[:, layer, 0, :], attn_row[:, layer, 1, :],
                           bias_col[:, 0, layer:layer + 1], 0.0 if layer == 0 else bias_col[:, 1, layer:layer + 1],
                           s_i, s_j).then_inc(s_ready.sem, 1)
                dve.wait_ge(s_ready.sem, s_ready.at(n))

            def final_norm(g, n, side):
                dve.wait_ge(x_ready.sem, x_ready.at(n))
                norm_stats(lambda c: x_res[:, side, c, :], lng_chain, g)
                norm_apply(lambda c: x_res[:, side, c, :], lng_rstd, g, lng_apply)

            def final_mask(g, side):
                dve.tensor_copy(mask_g[:, :, :], mask_t[:, side, :, :]).then_inc(mask_g_ready.sem, 1)
                dve.wait_ge(mask_g_ready.sem, mask_g_ready.at(g, 1))
                for c in range(NC):
                    last = dve.tensor_copy(mask_g[:, c, c * P:(c + 1) * P], diag_t[:, side, c, :])
                last.then_inc(mask_g_ready.sem, 1)
                dve.wait_ge(mask_g_ready.sem, mask_g_ready.at(g, 2))

            def final_scores(g):
                for c in range(NC):
                    dve.wait_ge(wh_copy.sem, wh_copy.at(g, c + 1))
                    dve.tensor_copy(sg_i[:, c:c + 1], ps_a[c % 2][:, D:D + 1])
                    dve.tensor_copy(sg_j[:, c:c + 1], ps_a[c % 2][:, D + 1:D + 2]).then_inc(sg_copy.sem, 1)
                dve.wait_ge(sg_copy.sem, sg_copy.at(g))
                dve.tensor_scalar(sg_j8[:, :], sg_j[:, :], 1.0 - SLOPE, None, ALU.mult)
                dve.tensor_scalar(sg_low[:, :], sg_i[:, :], SLOPE, None, ALU.mult).then_inc(sg_rows.sem, 1)
                dve.wait_ge(sg_rows.sem, sg_rows.at(g))

            def final_bounded(g, n):
                dve.wait_ge(g_low.sem, g_low.at(g))
                dve.wait_ge(g_rows.sem, g_rows.at(g, 1))
                dve.wait_ge(h_ready.sem, h_ready.at(n))
                def scores(j):
                    dve.scalar_tensor_tensor(out=probs[:, j, :], in0=ps_t[1][:, :], scalar=sg_j8[:, j:j + 1],
                                             in1=low_sb[:, :], op0=ALU.add, op1=ALU.max).then_inc(g_q.sem, 1)

                def negate(j):
                    dve.wait_ge(g_max.sem, g_max.at(g, j + 1))
                    dve.tensor_scalar(col_neg[:, j:j + 1], col_max[:, j:j + 1], -1.0, None, ALU.mult).then_inc(g_neg.sem, 1)

                scores(0)
                for j in range(NC):
                    dve.wait_ge(g_q.sem, g_q.at(g, j + 1))
                    if j + 1 < NC:
                        scores(j + 1)
                    else:
                        negate(j - 1)
                    dve.tensor_tensor_reduce(probs[:, j, :], probs[:, j, :], mask_g[:, j, :], 1.0,
                                             -3e38, ALU.add, ALU.max, col_max[:, j:j + 1]).then_inc(g_max.sem, 1)
                    if 1 <= j < NC - 1:
                        negate(j - 1)
                negate(NC - 1)

            def final_scale(g):
                dve.wait_ge(g_exp.sem, g_exp.at(g))
                dve.reciprocal(col_r[:, :], col_sum[:, :]).then_inc(g_r.sem, 1)
                dve.wait_ge(g_r.sem, g_r.at(g))
                for c in range(NC):
                    last = dve.tensor_scalar(wh[:, c, :], wh[:, c, :], col_r[:, c:c + 1], None, ALU.mult)
                last.then_inc(wh_scaled.sem, 1)

            def final_leaky(g):
                for c in range(NC):
                    dve.wait_ge(o_low.sem, o_low.at(g, c + 1))
                    dve.tensor_tensor(o_tmp[:, c % 2, :], ps_a[c % 2][:, 0:D], o_tmp[:, c % 2, :],
                                      ALU.max).then_inc(o_leaky.sem, 1)

            def parts(i):
                dve.wait_ge(weights_in[i % 2].sem, weights_in[i % 2].at(i // 2))
                _, hi, lo, _, _ = weight_loads[i]
                dve.tensor_copy(hi, staged(i)).then_inc(split_w.sem, 1)
                dve.wait_ge(split_w.sem, split_w.at(2 * i))
                dve.tensor_tensor(lo, staged(i), hi.bitcast(F32), ALU.subtract).then_inc(split_w.sem, 1)

            dve.wait_ge(loaded.sem, loaded.at(SMALL - 1))
            dve.wait_ge(consts.sem, consts.at(2))
            count = [0]

            def step(instruction):
                instruction.then_inc(setup_v.sem, 1)
                count[0] += 1
                dve.wait_ge(setup_v.sem, setup_v.at(count[0] - 1))

            step(dve.tensor_copy(ones_r[:, :], ones_f))
            step(dve.tensor_copy(ident_r[:, :], ident[:, :]))
            step(dve.tensor_copy(b2_round, b2_two))
            step(dve.scalar_tensor_tensor(out=b2_parts[:, :, :], in0=b2_round.bitcast(F32),
                                          scalar=minus_row[:, 0:1], in1=b2_two, op0=ALU.mult, op1=ALU.add))
            for l in range(1, LAYERS):
                for t in range(2):
                    step(dve.tensor_tensor_reduce(junk[:, 0:D], attn_row[:, l, t, :], beta2_row[:, l - 1, :], 1.0,
                                                  bias_col[:, 0, l:l + 1] if t == 0 else 0.0, ALU.mult, ALU.add,
                                                  bias_col[:, t, l:l + 1]))
                    step(dve.tensor_tensor(attn_row[:, l, t, :], attn_row[:, l, t, :], g2_row[:, l - 1, :], ALU.mult))

            for k in range(KC):
                for t in range(2):
                    step(dve.tensor_tensor_reduce(junk[:, D:2 * D], w_last[:, k, 0:D], a_row[:, t, :], 1.0, 0.0, ALU.mult,
                                                  ALU.add, w_last[:, k, D + t:D + t + 1]))
            assert count[0] == SETUP

            prepare_masks(0, 0)
            prepare_x(0, 0, 0)
            layer_scores(0, 0, 0)
            for i in range(len(weight_loads)):
                parts(i)
            dve.wait_ge(split_w.sem, split_w.at(2 * len(weight_loads) - 1))
            neighbour_max(0, 0)
            bounded_scores(0)
            attention_sum(0, 0)
            attention_norm(0)
            h_rest(0, 0)
            prepare_masks(1, 1)
            prepare_x(1, 1, 0)

            def pair_body(pair, first, last):
                for n, side, layer, final, prepare, attend, layer_a in slots(pair, first, last):
                    other = 1 - side
                    if not (first and side == 0 and layer == 0):
                        ff_norm(n - 1)
                    if side == 0 and layer == 0 and not first:
                        final_mask(pair * 2 - 1, 1)
                    if attend:
                        layer_scores(n + 1, layer_a, other)
                    for f in range(FC + LAG):
                        if f < FC and f % 2 == 1:
                            gelu_rest(n, f)
                        if f == 1 and layer == 0 and not first:
                            final_leaky(pair * 2 - 2 + side)
                        if f == 5 and layer == LAST and side == 0:
                            final_mask(pair * 2, 0)
                        if f == 6 and prepare is not None:
                            prepare_masks(prepare, side)
                            prepare_x(prepare, side, pair + 1)
                        if final is None:
                            if attend and f == 2:
                                neighbour_max(n + 1, other)
                            if attend and f == 3:
                                bounded_scores(n + 1, pair * 2 - 1 if layer == 0 and side == 1 and not first else None)
                            if attend and f == 5:
                                attention_sum(n + 1, other)
                                attention_norm(n + 1)
                            if attend and f == 8:
                                h_rest(n + 1, other)
                        else:
                            if attend and f == 1:
                                neighbour_max(n + 1, other)
                            if attend and f == 2:
                                bounded_scores(n + 1, None if side == 1 else final - 1)
                            if f == 3:
                                final_norm(final, n - 1, other)
                            if f == 5:
                                final_scores(final)
                            if attend and f == 6:
                                attention_sum(n + 1, other)
                                attention_norm(n + 1)
                            if f == 9:
                                if attend:
                                    h_rest(n + 1, other)
                                final_bounded(final, n + 1 if attend else n)
                                final_scale(final)

            each_pair(dve, pair_body)
            final_leaky(B - 2)
            ff_norm(B * LAYERS - 1)
            final_mask(B - 1, 1)
            final_norm(B - 1, B * LAYERS - 1, 1)
            final_scores(B - 1)
            final_bounded(B - 1, B * LAYERS - 1)
            final_scale(B - 1)
            final_leaky(B - 1)

        @block.gpsimd
        def _(pool):
            def inverse_root(chain, idx, done):
                pool.wait_ge(chain.sem, chain.at(idx))
                pool.tensor_tensor(rstd[:, :], var_eps[:, :], minus_half[:, :], ALU.pow).then_inc(done.sem, 1)

            def layer_input(n, side, layer):
                pool.wait_ge(ln2_apply.sem, ln2_apply.at(n))
                row = g2_row[:, layer:layer + 1, :].broadcast_to([P, NC, D])
                if layer < LAST:
                    target = x_nat[:, side, :, 0:D]
                    pool.tensor_tensor(target, normed[:, :, :], row, ALU.mult).then_inc(x_scaled.sem, 1)
                    pool.wait_ge(x_scaled.sem, x_scaled.at(n))
                    shift = beta2_row[:, layer:layer + 1, :].broadcast_to([P, NC, D])
                    pool.tensor_tensor(target, target, shift, ALU.add).then_inc(x_ready.sem, 1)
                else:
                    pool.tensor_tensor(normed[:, :, :], normed[:, :, :], row, ALU.mult).then_inc(x_scaled.sem, 1)
                    pool.wait_ge(x_scaled.sem, x_scaled.at(n))
                    pool.tensor_tensor(x_res[:, side, :, :], x_res[:, side, :, :], normed[:, :, :],
                                       ALU.add).then_inc(x_ready.sem, 1)

            def residual_shift(pair, side):
                g = pair * 2 + side
                pool.wait_ge(res_loaded[side].sem, res_loaded[side].at(pair))
                row = beta2_row[:, LAST:LAST + 1, :].broadcast_to([P, NC, D])
                pool.tensor_tensor(x_res[:, side, :, :], x_res[:, side, :, :], row, ALU.add).then_inc(res_beta.sem, 1)
                pool.wait_ge(res_beta.sem, res_beta.at(g))

            def gelu_rest(n, f):
                pool.wait_ge(gelu_done.sem, gelu_done.at(n, f + 1))
                pool.tensor_tensor(gelu_lo[:, f % RING, :], g_full[:, 0, :],
                                   gelu_hi[:, f % RING, :].bitcast(F32), ALU.subtract).then_inc(lo_done[0].sem, 1)

            def mask_scores(n, side):
                for j in range(NC):
                    pool.wait_ge(q_ready.sem, q_ready.at(n, j + 1))
                    pool.tensor_tensor(probs[:, j, :], probs[:, j, :], mask_t[:, side, j, :], ALU.add).then_inc(q_masked.sem, 1)

            def final_add(g, side):
                for c in range(NC):
                    pool.wait_ge(o_leaky.sem, o_leaky.at(g, c + 1))
                    pool.tensor_tensor(x_res[:, side, c, :], x_res[:, side, c, :], o_tmp[:, c % 2, :],
                                       ALU.add).then_inc(o_ready.sem, 1)

            pool.memset(ident[:, :], 0.0)
            pool.memset(ones_f, 1.0)
            pool.memset(minus_half[:, :], -0.5)
            pool.memset(minus_row[:, :], -1.0)
            pool.memset(x_nat[:, :, :, D:D + 1], 1.0).then_inc(consts.sem, 1)
            pool.wait_ge(consts.sem, consts.at(0))
            pool.affine_select(out=minus_row[:, :], in_=minus_row[:, :], compare_op=ALU.not_equal, fill=0.0,
                               base=0, pattern=[[0, 1]], channel_multiplier=1)
            pool.affine_select(out=ident[:, :], in_=ident[:, :], compare_op=ALU.not_equal, fill=1.0,
                               base=0, pattern=[[-1, P]], channel_multiplier=1).then_inc(consts.sem, 1)
            pool.wait_ge(consts.sem, consts.at(1))
            pool.tensor_copy(ident_b[:, :], ident[:, :]).then_inc(consts.sem, 1)
            inverse_root(ln0_chain, 0, ln0_rstd)
            mask_scores(0, 0)
            inverse_root(ln1_chain, 0, ln1_rstd)
            inverse_root(ln0_chain, 1, ln0_rstd)

            def pair_body(pair, first, last):
                for n, side, layer, final, prepare, attend, layer_a in slots(pair, first, last):
                    other = 1 - side
                    if not (first and side == 0 and layer == 0):
                        inverse_root(ln2_chain, n - 1, ln2_rstd)
                        layer_f = LAST if final is not None else layer - 1 + side
                        layer_input(n - 1, other, layer_f)
                    for f in range(FC + LAG):
                        if f < FC and f % 2 == 0:
                            gelu_rest(n, f)
                        if f == 1 and layer == 0 and not first:
                            final_add(pair * 2 - 2 + side, side)
                        if f == 4 and layer == LAST:
                            residual_shift(pair, side)
                        if f == 6 and prepare is not None:
                            inverse_root(ln0_chain, prepare, ln0_rstd)
                        if final is None:
                            if attend and f == 3:
                                mask_scores(n + 1, other)
                            if attend and f == 5:
                                inverse_root(ln1_chain, n + 1, ln1_rstd)
                        else:
                            if attend and f == 2:
                                mask_scores(n + 1, other)
                            if f == 3:
                                inverse_root(lng_chain, final, lng_rstd)
                            if attend and f == 6:
                                inverse_root(ln1_chain, n + 1, ln1_rstd)

            each_pair(pool, pair_body)
            final_add(B - 2, 0)
            inverse_root(ln2_chain, B * LAYERS - 1, ln2_rstd)
            layer_input(B * LAYERS - 1, 1, LAST)
            inverse_root(lng_chain, B - 1, lng_rstd)
            final_add(B - 1, 1)


_INS = ["x", "adj", "L0_gnn_attn_w", "L0_gnn_attn_b", "L0_gnn_W1", "L0_gnn_b1", "L0_gnn_W2", "L0_gnn_b2",
        "L0_gnn_g1", "L0_gnn_beta1", "L0_gnn_g2", "L0_gnn_beta2", "L1_gnn_W", "L1_gnn_a"]


def kernel(**inputs):
    import numpy as np
    import concourse.bacc as bacc
    from concourse.bass_utils import run_bass_kernel_spmd

    nc = bacc.Bacc("TRN2", target_bir_lowering=False, num_devices=1)
    arrays, args = {}, []
    for name in _INS:
        array = np.ascontiguousarray(inputs[name])
        arrays[f"{name}_dram"] = array
        args.append(nc.dram_tensor(f"{name}_dram", array.shape, mybir.dt.from_np(array.dtype),
                                   kind="ExternalInput").ap())
    out = nc.dram_tensor("out_dram", arrays["x_dram"].shape, F32, kind="ExternalOutput").ap()
    gnn_program(nc, *args, out)
    result = run_bass_kernel_spmd(nc, [arrays], core_ids=[0])
    return result.results[0]["out_dram"]
```

```python
from contextlib import ExitStack

import concourse.bass as bass
from concourse import mybir

F32 = mybir.dt.float32
F32R = mybir.dt.float32r
BF16 = mybir.dt.bfloat16
I32 = mybir.dt.int32
ALU = mybir.AluOpType
ACT = mybir.ActivationFunctionType

P = 128
EPS = 1e-5
SLOPE = 0.2
MASKED = -1e30



class Counted:

    def __init__(self, sem, per, unit):
        self.sem, self.per, self.unit = sem, per, unit

    def at(self, step, k=None):
        return step * (self.per * self.unit) + (self.per if k is None else k) * self.unit


def begun(value):
    return not isinstance(value, int) or value > 0


def gnn_program(nc, x, adj, attn_w, attn_b, W1, b1, W2, b2, g1, beta1, g2, beta2, Wl, al, out):
    B, N, D = x.shape
    LAYERS, _, F = W1.shape
    NC = N // P
    KC = D // P
    FC = F // P
    STEPS = 2 * LAYERS
    PAIRS = B // 2
    RING = 3
    LAST = LAYERS - 1
    BY_VECTOR = (1, 3, 4)
    BY_POOL = tuple(f for f in range(FC) if f not in BY_VECTOR)
    POOL_MASKED = NC - 1

    def lo_turn(f):
        return (1, BY_VECTOR.index(f) + 1) if f in BY_VECTOR else (0, BY_POOL.index(f) + 1)

    with ExitStack() as ctx:
        def sb(name, shape, dt):
            return ctx.enter_context(nc.sbuf_tensor(name, shape, dt))

        def sem(name, per=1, unit=1):
            return Counted(ctx.enter_context(nc.semaphore(name)), per, unit)

        w1_hi = sb("w1_hi", [P, LAYERS, KC, F], F32R)
        w1_lo = sb("w1_lo", [P, LAYERS, KC, F], F32R)
        w2_hi = sb("w2_hi", [P, LAYERS, FC, D], F32R)
        w2_lo = sb("w2_lo", [P, LAYERS, FC, D], F32R)
        w_last = sb("w_last", [P, KC, D + 2], F32)
        VECS = LAYERS * (FC + 2 * KC)
        vec_col = sb("vec_col", [P, VECS], F32)
        b1_col = vec_col[:, 0:LAYERS * FC].rearrange("p (l c) -> p l c", l=LAYERS)
        g1_col = vec_col[:, LAYERS * FC:LAYERS * (FC + KC)].rearrange("p (l c) -> p l c", l=LAYERS)
        beta1_col = vec_col[:, LAYERS * (FC + KC):VECS].rearrange("p (l c) -> p l c", l=LAYERS)
        attn_row = sb("attn_row", [P, LAYERS, 2, D], F32)
        g2_row = sb("g2_row", [P, LAYERS, D], F32)
        beta2_row = sb("beta2_row", [P, LAYERS, D], F32)
        bias_col = sb("bias_col", [P, 2, LAYERS], F32)
        b2_parts = sb("b2_parts", [2, LAYERS, D], F32R)
        minus_row = sb("minus_row", [2, 1], F32)
        ones_r = sb("ones_r", [2, P], F32R)
        ident = sb("ident", [P, P], F32)
        ident_r = sb("ident_r", [P, P], F32R)
        ident_b = sb("ident_b", [P, P], BF16)
        minus_half = sb("minus_half", [P, NC], F32)
        x_nat = sb("x_nat", [P, 2, NC, D + 1], F32)
        h_hi = sb("h_hi", [P, KC, N], F32R)
        h_lo = sb("h_lo", [P, KC, N], F32R)
        mask_nat = sb("mask_nat", [P, 2, NC, N], BF16)
        mask_t = sb("mask_t", [P, 2, NC, N], BF16)
        diag_t = sb("diag_t", [P, 2, NC, P], BF16)
        diag_nat = sb("diag_nat", [P, NC, P], BF16)
        adj_in = sb("adj_in", [P, 2, N], I32)
        adj_self = sb("adj_self", [P, P], F32)
        x_res = sb("x_res", [P, 2, NC, D], F32)
        mask_g = sb("mask_g", [P, NC, N], BF16)
        probs = sb("probs", [P, NC, N], F32)
        g_full = sb("g_full", [P, 2, N], F32)
        gelu_hi = sb("gelu_hi", [P, RING, N], F32R)
        gelu_lo = sb("gelu_lo", [P, RING, N], F32R)
        normed = sb("normed", [P, NC, D], F32)
        wh = sb("wh", [P, NC, D + 2], F32)
        h_last = sb("h_last", [P, KC, N], F32)
        stats = sb("stats", [P, NC, 6], F32)
        mean_sum = sb("mean_sum", [P, NC], F32)
        mean_gap = sb("mean_gap", [P, NC], F32)
        squares = sb("squares", [P, NC], F32)
        gap_sq = sb("gap_sq", [P, NC], F32)
        mean = sb("mean", [P, NC], F32)
        var_eps = sb("var_eps", [P, NC], F32)
        rstd = sb("rstd", [P, NC], F32)
        s_i = sb("s_i", [P, NC], F32)
        s_j = sb("s_j", [P, NC], F32)
        s_j8 = sb("s_j8", [P, NC], F32)
        s_j2 = sb("s_j2", [P, NC], F32)
        s_max = sb("s_max", [P, NC], F32)
        sg_j8 = sb("sg_j8", [P, NC], F32)
        x0_shift = sb("x0_shift", [P, NC], F32)
        o_tmp = sb("o_tmp", [P, 2, D], F32)
        low_sb = sb("low_sb", [P, N], F32)
        top = sb("top", [P, NC], F32)
        high = sb("high", [P, NC], F32)
        low = sb("low", [P, NC], F32)
        r_sum = sb("r_sum", [P, NC], F32)
        col_max = sb("col_max", [P, NC], F32)
        col_neg = sb("col_neg", [P, NC], F32)
        col_sum = sb("col_sum", [P, NC], F32)
        col_r = sb("col_r", [P, NC], F32)

        h_full = h_last
        junk = h_last[:, :, :].rearrange("p k n -> p (k n)").bitcast(BF16)
        vec_rows = o_tmp[0:VECS, 0, 0:P]
        a_row = normed[:, 0:2, :]
        b2_two = wh[0:2, 0:LAYERS, 0:D]
        ones_f = wh[0:2, LAYERS, 0:P]
        b2_round = h_last[0:2, :, :].rearrange("p k n -> p (k n)")[:, 0:LAYERS * D].bitcast(F32R).rearrange(
            "p (l d) -> p l d", l=LAYERS)

        def bank(name):
            return ctx.enter_context(nc.psum_tensor(name, [P, 512], F32))

        ps_u = [bank("ps_u0"), bank("ps_u1")]
        ps_d = [bank("ps_d0"), bank("ps_d1")]
        ps_a = [bank("ps_a0"), bank("ps_a1")]
        ps_t = [bank("ps_t0"), bank("ps_t1")]

        loaded = sem("loaded", 1, 16)
        weights_in = [sem(f"weights_in{i}", 1, 16) for i in range(2)]
        consts = sem("consts")
        split_w = sem("split_w")
        vec_tr = sem("vec_tr")
        vec_ready = sem("vec_ready")
        setup_v = sem("setup_v")
        x_loaded = [sem(f"x_loaded{side}", 1, 16) for side in range(2)]
        adj_loaded = [sem(f"adj_loaded{i}", NC // 2, 16) for i in range(2)]
        ln0_chain = sem("ln0_chain", 4)
        ln0_rstd = sem("ln0_rstd")
        ln0_shift = sem("ln0_shift")
        x0_ready = sem("x0_ready")
        self_added = sem("self_added", NC)
        nat_ready = sem("nat_ready", NC)
        mask_pe = sem("mask_pe", NC + 1)
        mask_ready = sem("mask_ready", NC + 1)
        s_ready = sem("s_ready")
        sj_bc = sem("sj_bc")
        max_ready = sem("max_ready")
        row_chain = sem("row_chain", 3)
        rows_bc = sem("rows_bc", 2)
        low_ready = sem("low_ready")
        q_ready = sem("q_ready", NC)
        q_masked = [sem("q_masked0", POOL_MASKED), sem("q_masked1", NC - POOL_MASKED)]
        p_ready = sem("p_ready", NC)
        agg_done = sem("agg_done", NC)
        rsum_ready = sem("rsum_ready", NC)
        y_ready = sem("y_ready", NC)
        ln1_chain = sem("ln1_chain", 4)
        ln1_rstd = sem("ln1_rstd")
        ln1_apply = sem("ln1_apply")
        h_tr = sem("h_tr", KC)
        hi_ready = sem("hi_ready", KC)
        h_act = sem("h_act", KC)
        h_ready = sem("h_ready", KC)
        u_done = sem("u_done", FC)
        gelu_done = sem("gelu_done", FC)
        lo_done = [sem("lo_done0", len(BY_POOL)), sem("lo_done1", len(BY_VECTOR))]
        d_used = sem("d_used", FC - 1)
        d_done = sem("d_done", 2)
        ln2_chain = sem("ln2_chain", 4)
        ln2_rstd = sem("ln2_rstd")
        ln2_apply = sem("ln2_apply", 2)
        x_scaled = sem("x_scaled")
        x_ready = sem("x_ready")
        res_loaded = [sem(f"res_loaded{side}", 1, 16) for side in range(2)]
        res_beta = sem("res_beta")
        lng_chain = sem("lng_chain", 4)
        lng_rstd = sem("lng_rstd")
        lng_apply = sem("lng_apply")
        g_tr = sem("g_tr", KC)
        g_act = sem("g_act", KC)
        wh_done = sem("wh_done", NC)
        wh_copy = sem("wh_copy", NC)
        sg_scaled = sem("sg_scaled")
        mask_g_ready = sem("mask_g_ready", 2)
        g_rows = sem("g_rows")
        g_low = sem("g_low")
        g_q = sem("g_q", NC)
        g_max = sem("g_max", NC)
        g_neg = sem("g_neg", NC)
        g_exp = sem("g_exp", NC)
        g_r = sem("g_r")
        wh_scaled = sem("wh_scaled")
        o_done = sem("o_done", NC)
        o_low = sem("o_low", NC)
        o_leaky = sem("o_leaky", NC)
        o_ready = sem("o_ready", NC)
        stored = [sem(f"stored{side}", NC, 16) for side in range(2)]

        block = ctx.enter_context(nc.Block())

        stage = [probs[:, :, :].rearrange("p c n -> p (c n)"), x_res[:, :, :, :].rearrange("p s c d -> p (s c d)")]
        weight_loads = []
        for l in range(LAYERS):
            weight_loads.append((W1[l].rearrange("(k p) f -> p k f", p=P), w1_hi[:, l], w1_lo[:, l], KC, F))
            weight_loads.append((W2[l].rearrange("(k p) f -> p k f", p=P), w2_hi[:, l], w2_lo[:, l], FC, D))
        SETUP = 4 + 4 * (LAYERS - 1) + 2 * KC
        SMALL = 10

        def staged(i):
            _, _, _, k, n = weight_loads[i]
            return stage[i % 2][:, 0:k * n].rearrange("p (k n) -> p k n", k=k)

        def each_pair(engine, body):
            body(0, True, PAIRS == 1)
            if PAIRS > 2:
                with engine.Fori(1, PAIRS - 1) as pair:
                    body(pair, False, False)
            if PAIRS > 1:
                body(PAIRS - 1, False, True)

        def slots(pair, first, last):
            for layer in range(LAYERS):
                for side in range(2):
                    n = pair * STEPS + 2 * layer + side
                    final = None
                    if side == 1 and layer == LAST:
                        final = pair * 2
                    if side == 0 and layer == 0 and not first:
                        final = pair * 2 - 1
                    prepare = pair * 2 + 2 + side if layer == LAST and not last else None
                    attend = not (side == 1 and layer == LAST and last)
                    yield n, side, layer, final, prepare, attend, (layer + side) % LAYERS

        @block.sync
        def _(sp):
            small = [
                (vec_rows[0:LAYERS * FC, :], b1.rearrange("l (c p) -> (l c) p", p=P)),
                (vec_rows[LAYERS * FC:LAYERS * (FC + KC), :], g1.rearrange("l (c p) -> (l c) p", p=P)),
                (vec_rows[LAYERS * (FC + KC):VECS, :], beta1.rearrange("l (c p) -> (l c) p", p=P)),
                (attn_row[:, :, :, :], attn_w.rearrange("(o l) (t d) -> o l t d", o=1, t=2).broadcast_to([P, LAYERS, 2, D])),
                (w_last[:, :, 0:D], Wl.rearrange("(k p) f -> p k f", p=P)),
                (a_row, al.rearrange("(t d) o -> o t d", t=2).broadcast_to([P, 2, D])),
                (g2_row[:, :, :], g2.rearrange("(o l) d -> o l d", o=1).broadcast_to([P, LAYERS, D])),
                (beta2_row[:, :, :], beta2.rearrange("(o l) d -> o l d", o=1).broadcast_to([P, LAYERS, D])),
                (b2_two, b2.rearrange("(o l) d -> o l d", o=1).broadcast_to([2, LAYERS, D])),
                (bias_col[:, 0, :], attn_b.rearrange("(o l) -> o l", o=1).broadcast_to([P, LAYERS])),
            ]
            assert len(small) == SMALL

            def load_input(g, side, step_before):
                if step_before is not None:
                    sp.wait_ge(y_ready.sem, y_ready.at(step_before))
                sp.dma_start(x_nat[:, side, :, 0:D], x[g].rearrange("(c p) d -> p c d", p=P)).then_inc(x_loaded[side].sem, 16)
                for c in range(NC):
                    if begun(self_added.at(g, c - 1)):
                        sp.wait_ge(self_added.sem, self_added.at(g, c - 1))
                    sp.dma_start(adj_in[:, c % 2, :], adj[g][c * P:(c + 1) * P, :]).then_inc(adj_loaded[c % 2].sem, 16)

            def load_residual(pair, side):
                g = pair * 2 + side
                if begun(stored[side].at(pair - 1)):
                    sp.wait_ge(stored[side].sem, stored[side].at(pair - 1))
                sp.dma_start(x_res[:, side, :, :], x[g].rearrange("(c p) d -> p c d", p=P)).then_inc(res_loaded[side].sem, 16)

            def store(g, side):
                for c in range(NC):
                    sp.wait_ge(o_ready.sem, o_ready.at(g, c + 1))
                    sp.dma_start(out[g][c * P:(c + 1) * P, :], x_res[:, side, c, :]).then_inc(stored[side].sem, 16)

            for dst, src in small:
                sp.dma_start(dst, src).then_inc(loaded.sem, 16)
            sp.wait_ge(consts.sem, consts.at(0))
            load_input(0, 0, None)
            for i, (src, _, _, _, _) in enumerate(weight_loads):
                if begun(split_w.at(2 * i - 3)):
                    sp.wait_ge(split_w.sem, split_w.at(2 * i - 3))
                sp.dma_start(staged(i), src).then_inc(weights_in[i % 2].sem, 16)
            load_input(1, 1, None)

            def pair_body(pair, first, last):
                for n, side, layer, final, prepare, attend, _ in slots(pair, first, last):
                    if layer == 0 and not first:
                        store(pair * 2 - 2 + side, side)
                    if layer == LAST:
                        load_residual(pair, side)
                    if prepare is not None:
                        load_input(prepare, side, n)

            each_pair(sp, pair_body)
            for side in range(2):
                store(B - 2 + side, side)
            for side in range(2):
                sp.wait_ge(stored[side].sem, stored[side].at(PAIRS - 1))

        @block.tensor
        def _(pe):
            def columns_to_rows(dst, col):
                for c in range(NC):
                    last = pe.transpose(dst[:, c * P:(c + 1) * P], col[:, c:c + 1].broadcast_to([P, P]),
                                        ident[:, :])
                return last

            def mask_transposes(g, side, chunks):
                for c in chunks:
                    view = ps_t[c % 2][:, :].bitcast(BF16)
                    if c >= 2:
                        pe.wait_ge(mask_ready.sem, mask_ready.at(g, c - 1))
                    if c < NC:
                        pe.wait_ge(nat_ready.sem, nat_ready.at(g, c + 1))
                    for j in range(NC):
                        block = mask_nat[:, side, c, j * P:(j + 1) * P] if c < NC else diag_nat[:, j, :]
                        last = pe.transpose(view[:, j * P:(j + 1) * P], block, ident_b[:, :])
                    last.then_inc(mask_pe.sem, 1)

            def scores_row(n):
                pe.wait_ge(s_ready.sem, s_ready.at(n))
                columns_to_rows(ps_t[0], s_j).then_inc(sj_bc.sem, 1)

            def bound_rows(n):
                pe.wait_ge(row_chain.sem, row_chain.at(n))
                columns_to_rows(ps_t[0], low).then_inc(rows_bc.sem, 1)
                columns_to_rows(ps_t[1], high).then_inc(rows_bc.sem, 1)

            def attend_out(n, side, layer, g, late):
                if layer == 0:
                    pe.wait_ge(x0_ready.sem, x0_ready.at(g))
                else:
                    pe.wait_ge(x_ready.sem, x_ready.at(n - 2))
                for c in range(NC):
                    if c >= 2:
                        pe.wait_ge(y_ready.sem, y_ready.at(n, c - 1))
                    elif late is not None:
                        pe.wait_ge(o_leaky.sem, o_leaky.at(late, NC - 1 + c))
                    elif begun(y_ready.at(n - 1)):
                        pe.wait_ge(y_ready.sem, y_ready.at(n - 1))
                    for j in range(NC):
                        if c == 0:
                            pe.wait_ge(p_ready.sem, p_ready.at(n, j + 1))
                        last = pe.matmul(ps_a[c % 2][:, 0:D + 1], probs[:, j, c * P:(c + 1) * P], x_nat[:, side, j, :],
                                         start=(j == 0), stop=(j == NC - 1))
                    last.then_inc(agg_done.sem, 1)

            def turn_tokens(applied, turned, step):
                pe.wait_ge(applied.sem, applied.at(step))
                for k in range(KC):
                    for c in range(NC):
                        last = pe.transpose(ps_t[k][:, c * P:(c + 1) * P], normed[:, c, k * P:(k + 1) * P], ident[:, :])
                    last.then_inc(turned.sem, 1)

            def up_first(n, layer):
                for k in range(KC):
                    pe.wait_ge(hi_ready.sem, hi_ready.at(n, k + 1))
                    for f in range(2):
                        if k == 0 and begun(gelu_done.at(n, f - 1)):
                            pe.wait_ge(gelu_done.sem, gelu_done.at(n, f - 1))
                        lhs = slice(f * P, (f + 1) * P)
                        pe.matmul(ps_u[f][:, :], w1_hi[:, layer, k, lhs], h_hi[:, k, :], start=(k == 0), stop=False)
                        pe.matmul(ps_u[f][:, :], w1_lo[:, layer, k, lhs], h_hi[:, k, :], start=False, stop=False)
                for f in range(2):
                    lhs = slice(f * P, (f + 1) * P)
                    for k in range(KC):
                        pe.wait_ge(h_ready.sem, h_ready.at(n, k + 1))
                        last = pe.matmul(ps_u[f][:, :], w1_hi[:, layer, k, lhs], h_lo[:, k, :],
                                         start=False, stop=(k == KC - 1))
                    last.then_inc(u_done.sem, 1)

            def up(n, layer, f):
                pe.wait_ge(gelu_done.sem, gelu_done.at(n, f - 1))
                lhs = slice(f * P, (f + 1) * P)
                terms = [(w, h, k) for k in range(KC) for w, h in ((w1_hi, h_hi), (w1_hi, h_lo), (w1_lo, h_hi))]
                for i, (w, h, k) in enumerate(terms):
                    last = pe.matmul(ps_u[f % 2][:, :], w[:, layer, k, lhs], h[:, k, :],
                                     start=(i == 0), stop=(i == len(terms) - 1))
                last.then_inc(u_done.sem, 1)

            def residual(n, layer):
                for c in range(NC):
                    if c % 2 == 0 and begun(ln2_apply.at(n - 1)):
                        pe.wait_ge(ln2_apply.sem, ln2_apply.at(n - 1, c // 2 + 1))
                    cols = (c % 2) * D
                    dst = ps_d[c // 2]
                    for k in range(KC):
                        for i, h in enumerate((h_hi, h_lo)):
                            pe.matmul(dst[:, cols + k * P:cols + (k + 1) * P], h[:, k, c * P:(c + 1) * P],
                                      ident_r[:, :], start=(c % 2 == 0 and k == 0 and i == 0), stop=False,
                                      skip_group_check=True)
                    pe.matmul(dst[:, cols:cols + D], ones_r[:, :], b2_parts[:, layer, :], start=False, stop=False,
                              skip_group_check=True)

            def down(n, layer, f):
                if f == 0:
                    residual(n, layer)
                by, turn = lo_turn(f)
                pe.wait_ge(lo_done[by].sem, lo_done[by].at(n, turn))
                r = f % RING
                for c in range(NC):
                    cols = (c % 2) * D
                    tok = slice(c * P, (c + 1) * P)
                    for i, (h, w) in enumerate(((gelu_hi, w2_hi), (gelu_hi, w2_lo), (gelu_lo, w2_hi))):
                        last = pe.matmul(ps_d[c // 2][:, cols:cols + D], h[:, r, tok], w[:, layer, f, :],
                                         start=False, stop=(f == FC - 1 and i == 2), skip_group_check=True)
                    if f == FC - 1 and c % 2 == 1:
                        last.then_inc(d_done.sem, 1)
                    if f < FC - 1 and c == NC - 1:
                        last.then_inc(d_used.sem, 1)

            def project(g, n):
                pe.wait_ge(g_act.sem, g_act.at(g))
                for c in range(NC):
                    if c >= 2:
                        pe.wait_ge(wh_copy.sem, wh_copy.at(g, c - 1))
                    else:
                        pe.wait_ge(y_ready.sem, y_ready.at(n, NC - 1 + c))
                    for k in range(KC):
                        last = pe.matmul(ps_a[c % 2][:, 0:D + 2], h_last[:, k, c * P:(c + 1) * P], w_last[:, k, :],
                                         start=(k == 0), stop=(k == KC - 1))
                    last.then_inc(wh_done.sem, 1)

            def final_rows(g):
                pe.wait_ge(wh_copy.sem, wh_copy.at(g))
                columns_to_rows(ps_a[1], wh[:, :, D]).then_inc(g_rows.sem, 1)

            def final_out(g, chunks):
                pe.wait_ge(wh_scaled.sem, wh_scaled.at(g))
                for c in chunks:
                    if c >= 2:
                        pe.wait_ge(o_leaky.sem, o_leaky.at(g, c - 1))
                    for j in range(NC):
                        last = pe.matmul(ps_a[c % 2][:, 0:D], probs[:, j, c * P:(c + 1) * P], wh[:, j, 0:D],
                                         start=(j == 0), stop=(j == NC - 1))
                    last.then_inc(o_done.sem, 1)

            pe.wait_ge(consts.sem, consts.at(2))
            pe.wait_ge(loaded.sem, loaded.at(SMALL - 1))
            pe.transpose(ps_t[0][:, 0:VECS], vec_rows, ident[0:VECS, 0:VECS]).then_inc(vec_tr.sem, 1)
            pe.wait_ge(vec_ready.sem, vec_ready.at(0))
            mask_transposes(0, 0, range(NC + 1))
            pe.wait_ge(mask_ready.sem, mask_ready.at(0, NC + 1))
            scores_row(0)
            bound_rows(0)
            attend_out(0, 0, 0, 0, None)
            turn_tokens(ln1_apply, h_tr, 0)
            pe.wait_ge(h_act.sem, h_act.at(0))
            mask_transposes(1, 1, range(NC + 1))
            pe.wait_ge(split_w.sem, split_w.at(2 * len(weight_loads) - 1))
            pe.wait_ge(setup_v.sem, setup_v.at(SETUP - 1))

            def regular_slot(n, side, layer, late, prepare, graph_a, layer_a):
                up_first(n, layer)
                up(n, layer, 2)
                up(n, layer, 3)
                down(n, layer, 0)
                if isinstance(n, int) and n == 0:
                    pe.wait_ge(mask_ready.sem, mask_ready.at(1, NC + 1))
                else:
                    pe.wait_ge(h_act.sem, h_act.at(n))
                if late is None:
                    scores_row(n + 1)
                down(n, layer, 1)
                if late is not None:
                    final_out(late, (0, 1))
                    scores_row(n + 1)
                    final_out(late, (2, 3))
                up(n, layer, 4)
                down(n, layer, 2)
                bound_rows(n + 1)
                up(n, layer, 5)
                down(n, layer, 3)
                up(n, layer, 6)
                down(n, layer, 4)
                attend_out(n + 1, 1 - side, layer_a, graph_a, late)
                pe.wait_ge(q_ready.sem, q_ready.at(n + 1))
                if prepare is not None:
                    mask_transposes(prepare, 0, (0, 1))
                up(n, layer, 7)
                if prepare is not None:
                    mask_transposes(prepare, 0, (2, 3))
                down(n, layer, 5)
                if prepare is not None:
                    mask_transposes(prepare, 0, (4,))
                down(n, layer, 6)
                if prepare is not None:
                    pe.wait_ge(mask_ready.sem, mask_ready.at(prepare, NC + 1))
                turn_tokens(ln1_apply, h_tr, n + 1)
                down(n, layer, 7)

            def final_slot(n, side, layer, final, late, attend, graph_a, layer_a):
                up_first(n, layer)
                pe.wait_ge(h_act.sem, h_act.at(n))
                if late is not None:
                    mask_transposes(graph_a, 1, (0, 1))
                up(n, layer, 2)
                if late is not None:
                    mask_transposes(graph_a, 1, (2, 3))
                up(n, layer, 3)
                down(n, layer, 0)
                down(n, layer, 1)
                if late is not None:
                    mask_transposes(graph_a, 1, (4,))
                    final_out(late, range(NC))
                    pe.wait_ge(mask_ready.sem, mask_ready.at(graph_a, NC + 1))
                    scores_row(n + 1)
                up(n, layer, 4)
                down(n, layer, 2)
                if attend and late is None:
                    scores_row(n + 1)
                up(n, layer, 5)
                down(n, layer, 3)
                if attend:
                    bound_rows(n + 1)
                up(n, layer, 6)
                if attend:
                    pe.wait_ge(q_ready.sem, q_ready.at(n + 1))
                turn_tokens(lng_apply, g_tr, final)
                down(n, layer, 4)
                if attend:
                    attend_out(n + 1, 1 - side, layer_a, graph_a, late)
                project(final, n + 1 if attend else n)
                final_rows(final)
                up(n, layer, 7)
                down(n, layer, 5)
                down(n, layer, 6)
                if attend:
                    turn_tokens(ln1_apply, h_tr, n + 1)
                down(n, layer, 7)

            def pair_body(pair, first, last):
                for n, side, layer, final, prepare, attend, layer_a in slots(pair, first, last):
                    graph_a = pair * 2 + 1 if side == 0 else pair * 2 + 2
                    late = pair * 2 - 2 + side if layer == 0 and not first else None
                    if final is None:
                        regular_slot(n, side, layer, late, prepare if side == 0 else None, graph_a, layer_a)
                    else:
                        final_slot(n, side, layer, final, late, attend, graph_a, layer_a)

            each_pair(pe, pair_body)
            final_out(B - 2, range(NC))
            turn_tokens(lng_apply, g_tr, B - 1)
            pe.wait_ge(o_leaky.sem, o_leaky.at(B - 2))
            project(B - 1, B * LAYERS - 1)
            final_rows(B - 1)
            final_out(B - 1, range(NC))

        @block.scalar
        def _(act):
            def mask_copies(g, side, chunks):
                if begun(mask_g_ready.at(g - 2)):
                    act.wait_ge(mask_g_ready.sem, mask_g_ready.at(g - 2))
                for c in chunks:
                    act.wait_ge(mask_pe.sem, mask_pe.at(g, c + 1))
                    src = ps_t[c % 2][:, :].bitcast(BF16)[:, 0:N].rearrange("p (j i) -> p j i", i=P)
                    dst = mask_t[:, side, :, c * P:(c + 1) * P] if c < NC else diag_t[:, side, :, :]
                    act.activation(dst, src, ACT.Copy).then_inc(mask_ready.sem, 1)

            def input_apply(g, side):
                act.wait_ge(ln0_shift.sem, ln0_shift.at(g))
                for c in range(NC):
                    last = act.activation(x_nat[:, side, c, 0:D], x_nat[:, side, c, 0:D], ACT.Relu,
                                          bias=x0_shift[:, c:c + 1], scale=rstd[:, c:c + 1])
                last.then_inc(x0_ready.sem, 1)

            def low_row(n):
                act.wait_ge(rows_bc.sem, rows_bc.at(n, 1))
                act.activation(low_sb[:, :], ps_t[0][:, :], ACT.Copy).then_inc(low_ready.sem, 1)

            def exps(n):
                for j in range(NC):
                    if j < POOL_MASKED:
                        act.wait_ge(q_masked[0].sem, q_masked[0].at(n, j + 1))
                    else:
                        act.wait_ge(q_masked[1].sem, q_masked[1].at(n, j - POOL_MASKED + 1))
                    act.activation(probs[:, j, :], probs[:, j, :], ACT.Exp, bias=s_j2[:, j:j + 1]).then_inc(p_ready.sem, 1)

            def h_split(n, layer):
                for k in range(KC):
                    act.wait_ge(h_tr.sem, h_tr.at(n, k + 1))
                    act.activation(h_hi[:, k, :], ps_t[k][:, :], ACT.Identity,
                                   bias=beta1_col[:, layer, k:k + 1], scale=g1_col[:, layer, k:k + 1]).then_inc(hi_ready.sem, 1)
                    act.activation(h_full[:, k, :], ps_t[k][:, :], ACT.Identity, bias=beta1_col[:, layer, k:k + 1],
                                   scale=g1_col[:, layer, k:k + 1]).then_inc(h_act.sem, 1)

            def gelu(n, layer, f):
                act.wait_ge(u_done.sem, u_done.at(n, f + 1))
                by, turn = lo_turn((f - 2) % FC)
                step = n if f >= 2 else n - 1
                if begun(lo_done[by].at(step, turn)):
                    act.wait_ge(lo_done[by].sem, lo_done[by].at(step, turn))
                act.activation(g_full[:, f % 2, :], ps_u[f % 2][:, :], ACT.Gelu, bias=b1_col[:, layer, f:f + 1])
                if f >= RING:
                    act.wait_ge(d_used.sem, d_used.at(n, f - RING + 1))
                act.activation(gelu_hi[:, f % RING, :], ps_u[f % 2][:, :], ACT.Gelu,
                               bias=b1_col[:, layer, f:f + 1]).then_inc(gelu_done.sem, 1)

            def final_h(g):
                for k in range(KC):
                    act.wait_ge(g_tr.sem, g_tr.at(g, k + 1))
                    act.activation(h_last[:, k, :], ps_t[k][:, :], ACT.Relu).then_inc(g_act.sem, 1)

            def final_wh(g):
                for c in range(NC):
                    act.wait_ge(wh_done.sem, wh_done.at(g, c + 1))
                    act.activation(wh[:, c, :], ps_a[c % 2][:, 0:D + 2], ACT.Copy).then_inc(wh_copy.sem, 1)

            def final_low(g):
                act.wait_ge(g_rows.sem, g_rows.at(g))
                act.activation(low_sb[:, :], ps_a[1][:, :], ACT.Copy, scale=SLOPE).then_inc(g_low.sem, 1)

            def final_exps(g):
                for j in range(NC):
                    act.wait_ge(g_neg.sem, g_neg.at(g, j + 1))
                    act.activation(probs[:, j, :], probs[:, j, :], ACT.Exp, bias=col_neg[:, j:j + 1],
                                   accum_out=col_sum[:, j:j + 1]).then_inc(g_exp.sem, 1)

            act.wait_ge(vec_tr.sem, vec_tr.at(0))
            act.activation(vec_col[:, :], ps_t[0][:, 0:VECS], ACT.Copy).then_inc(vec_ready.sem, 1)
            act.wait_ge(vec_ready.sem, vec_ready.at(0))
            mask_copies(0, 0, range(NC + 1))
            input_apply(0, 0)
            low_row(0)
            exps(0)
            h_split(0, 0)
            mask_copies(1, 1, range(NC + 1))

            def pair_body(pair, first, last):
                for n, side, layer, final, prepare, attend, layer_a in slots(pair, first, last):
                    late = pair * 2 - 2 + side if layer == 0 and not first else None
                    masks_y = pair * 2 + 1 if side == 0 and late is not None else None
                    masks_x = prepare if side == 0 else None
                    gelu(n, layer, 0)
                    gelu(n, layer, 1)
                    if masks_y is not None:
                        mask_copies(masks_y, 1, (0, 1))
                    if late is not None:
                        final_exps(late)
                    gelu(n, layer, 2)
                    if masks_y is not None:
                        mask_copies(masks_y, 1, (2, 3))
                    if attend and layer_a == 0:
                        input_apply(pair * 2 + 1 + side, 1 - side)
                    gelu(n, layer, 3)
                    if masks_y is not None:
                        mask_copies(masks_y, 1, (4,))
                    gelu(n, layer, 4)
                    if attend:
                        low_row(n + 1)
                        exps(n + 1)
                    if final is not None:
                        final_h(final)
                    gelu(n, layer, 5)
                    gelu(n, layer, 6)
                    if final is not None:
                        final_wh(final)
                        final_low(final)
                    if masks_x is not None:
                        mask_copies(masks_x, 0, (0, 1))
                    gelu(n, layer, 7)
                    if masks_x is not None:
                        mask_copies(masks_x, 0, (2, 3, 4))
                    if attend:
                        h_split(n + 1, layer_a)

            each_pair(act, pair_body)
            final_exps(B - 2)
            final_h(B - 1)
            final_wh(B - 1)
            final_low(B - 1)
            final_exps(B - 1)

        @block.vector
        def _(dve):
            def norm_stats(source, chain, idx):
                for c in range(NC):
                    last = dve.bn_stats(stats[:, c, :], source(c))
                last.then_inc(chain.sem, 1)
                variance(chain, idx)

            def variance(chain, idx):
                dve.wait_ge(chain.sem, chain.at(idx, 1))
                dve.tensor_tensor(mean_sum[:, :], stats[:, :, 1], stats[:, :, 4], ALU.add)
                dve.tensor_tensor(mean_gap[:, :], stats[:, :, 1], stats[:, :, 4], ALU.subtract)
                dve.scalar_tensor_tensor(out=squares[:, :], in0=stats[:, :, 2], scalar=D * EPS,
                                         in1=stats[:, :, 5], op0=ALU.add, op1=ALU.add).then_inc(chain.sem, 1)
                dve.wait_ge(chain.sem, chain.at(idx, 2))
                dve.tensor_scalar(mean[:, :], mean_sum[:, :], 0.5, None, ALU.mult)
                dve.scalar_tensor_tensor(out=gap_sq[:, :], in0=mean_gap[:, :], scalar=0.25,
                                         in1=mean_gap[:, :], op0=ALU.mult, op1=ALU.mult).then_inc(chain.sem, 1)
                dve.wait_ge(chain.sem, chain.at(idx, 3))
                dve.scalar_tensor_tensor(out=var_eps[:, :], in0=squares[:, :], scalar=1.0 / D,
                                         in1=gap_sq[:, :], op0=ALU.mult, op1=ALU.add).then_inc(chain.sem, 1)

            def norm_apply(source, ready, idx, done):
                dve.wait_ge(ready.sem, ready.at(idx))
                for c in range(NC):
                    last = dve.tensor_scalar(normed[:, c, :], source(c), mean[:, c:c + 1], rstd[:, c:c + 1],
                                             ALU.subtract, ALU.mult)
                last.then_inc(done.sem, 1)
                dve.wait_ge(done.sem, done.at(idx))

            def prepare_masks(g, side):
                for c in range(NC):
                    blk = slice(c * P, (c + 1) * P)
                    dve.wait_ge(adj_loaded[c % 2].sem, adj_loaded[c % 2].at(g, c // 2 + 1))
                    dve.tensor_scalar(mask_nat[:, side, c, :], adj_in[:, c % 2, :], 0.0, MASKED, ALU.is_le, ALU.mult)
                    dve.tensor_scalar(diag_nat[:, c, :], adj_in[:, c % 2, blk], 0.0, MASKED, ALU.is_le, ALU.mult)
                    dve.tensor_tensor(adj_self[:, :], adj_in[:, c % 2, blk], ident[:, :], ALU.add).then_inc(self_added.sem, 1)
                    dve.wait_ge(self_added.sem, self_added.at(g, c + 1))
                    dve.tensor_scalar(mask_nat[:, side, c, blk], adj_self[:, :], 0.0, MASKED,
                                      ALU.is_le, ALU.mult).then_inc(nat_ready.sem, 1)
                    dve.wait_ge(nat_ready.sem, nat_ready.at(g, c + 1))

            def prepare_x(g, side, pair, meanwhile=None):
                dve.wait_ge(x_loaded[side].sem, x_loaded[side].at(pair))
                norm_stats(lambda c: x_nat[:, side, c, 0:D], ln0_chain, g)
                if meanwhile is not None:
                    gelu_rest(meanwhile, 1)
                dve.wait_ge(ln0_rstd.sem, ln0_rstd.at(g))
                dve.scalar_tensor_tensor(out=x0_shift[:, :], in0=mean[:, :], scalar=-1.0, in1=rstd[:, :],
                                         op0=ALU.mult, op1=ALU.mult).then_inc(ln0_shift.sem, 1)

            def token_dots(source, row_i, row_j, init_i, init_j, to_i, to_j):
                for c in range(NC):
                    dve.tensor_tensor_reduce(junk[:, 2 * c * D:(2 * c + 1) * D], source(c), row_i, 1.0, init_i,
                                             ALU.mult, ALU.add, to_i[:, c:c + 1])
                    last = dve.tensor_tensor_reduce(junk[:, (2 * c + 1) * D:(2 * c + 2) * D], source(c), row_j, 1.0,
                                                    init_j, ALU.mult, ALU.add, to_j[:, c:c + 1])
                return last

            def neighbour_max(n, side):
                dve.wait_ge(sj_bc.sem, sj_bc.at(n))
                dve.tensor_scalar(s_j8[:, :], s_j[:, :], 1.0 - SLOPE, None, ALU.mult)
                dve.tensor_scalar(s_j2[:, :], s_j[:, :], SLOPE, None, ALU.mult)
                for c in range(NC):
                    last = dve.tensor_tensor_reduce(junk[:, c * N:(c + 1) * N], ps_t[0][:, :], mask_nat[:, side, c, :],
                                                    1.0, -3e38, ALU.add, ALU.max, s_max[:, c:c + 1])
                last.then_inc(max_ready.sem, 1)
                dve.wait_ge(max_ready.sem, max_ready.at(n))
                dve.tensor_tensor(high[:, :], s_i[:, :], s_max[:, :], ALU.add).then_inc(row_chain.sem, 1)
                dve.wait_ge(row_chain.sem, row_chain.at(n, 1))
                dve.scalar_tensor_tensor(out=top[:, :], in0=high[:, :], scalar=SLOPE, in1=high[:, :],
                                         op0=ALU.mult, op1=ALU.max).then_inc(row_chain.sem, 1)
                dve.wait_ge(row_chain.sem, row_chain.at(n, 2))
                dve.tensor_tensor(high[:, :], s_i[:, :], top[:, :], ALU.subtract)
                dve.scalar_tensor_tensor(out=low[:, :], in0=s_i[:, :], scalar=SLOPE, in1=top[:, :],
                                         op0=ALU.mult, op1=ALU.subtract).then_inc(row_chain.sem, 1)

            def bounded_scores(n, side, graph_before=None):
                dve.wait_ge(low_ready.sem, low_ready.at(n))
                dve.wait_ge(rows_bc.sem, rows_bc.at(n))
                if begun(agg_done.at(n - 1)):
                    dve.wait_ge(agg_done.sem, agg_done.at(n - 1))
                if graph_before is not None:
                    dve.wait_ge(o_done.sem, o_done.at(graph_before))
                for j in range(NC):
                    dve.scalar_tensor_tensor(out=probs[:, j, :], in0=ps_t[1][:, :], scalar=s_j8[:, j:j + 1],
                                             in1=low_sb[:, :], op0=ALU.add, op1=ALU.max).then_inc(q_ready.sem, 1)
                for j in range(POOL_MASKED, NC):
                    dve.wait_ge(q_ready.sem, q_ready.at(n, j + 1))
                    dve.tensor_tensor(probs[:, j, :], probs[:, j, :], mask_t[:, side, j, :],
                                      ALU.add).then_inc(q_masked[1].sem, 1)

            def attention_sum(n, side):
                for c in range(NC):
                    dve.wait_ge(agg_done.sem, agg_done.at(n, c + 1))
                    dve.reciprocal(r_sum[:, c:c + 1], ps_a[c % 2][:, D:D + 1]).then_inc(rsum_ready.sem, 1)
                    dve.wait_ge(rsum_ready.sem, rsum_ready.at(n, c + 1))
                    dve.scalar_tensor_tensor(out=normed[:, c, :], in0=ps_a[c % 2][:, 0:D],
                                             scalar=r_sum[:, c:c + 1], in1=x_nat[:, side, c, 0:D],
                                             op0=ALU.mult, op1=ALU.add).then_inc(y_ready.sem, 1)
                    dve.wait_ge(y_ready.sem, y_ready.at(n, c + 1))
                    last = dve.bn_stats(stats[:, c, :], normed[:, c, :])
                last.then_inc(ln1_chain.sem, 1)
                variance(ln1_chain, n)

            def attention_norm(n):
                norm_apply(lambda c: normed[:, c, :], ln1_rstd, n, ln1_apply)

            def h_rest(n):
                for k in range(KC):
                    dve.wait_ge(h_act.sem, h_act.at(n, k + 1))
                    dve.tensor_tensor(h_lo[:, k, :], h_full[:, k, :],
                                      h_hi[:, k, :].bitcast(F32), ALU.subtract).then_inc(h_ready.sem, 1)
                dve.wait_ge(h_ready.sem, h_ready.at(n))

            def gelu_rest(n, f):
                dve.wait_ge(gelu_done.sem, gelu_done.at(n, f + 1))
                dve.tensor_tensor(gelu_lo[:, f % RING, :], g_full[:, f % 2, :],
                                  gelu_hi[:, f % RING, :].bitcast(F32), ALU.subtract).then_inc(lo_done[1].sem, 1)

            def ff_norm(n):
                def source(c):
                    return ps_d[c // 2][:, (c % 2) * D:(c % 2 + 1) * D]
                for c in range(NC):
                    if c % 2 == 0:
                        dve.wait_ge(d_done.sem, d_done.at(n, c // 2 + 1))
                    last = dve.bn_stats(stats[:, c, :], source(c))
                last.then_inc(ln2_chain.sem, 1)
                variance(ln2_chain, n)
                dve.wait_ge(ln2_rstd.sem, ln2_rstd.at(n))
                for c in range(NC):
                    last = dve.tensor_scalar(normed[:, c, :], source(c), mean[:, c:c + 1], rstd[:, c:c + 1],
                                             ALU.subtract, ALU.mult)
                    if c % 2 == 1:
                        last.then_inc(ln2_apply.sem, 1)
                dve.wait_ge(ln2_apply.sem, ln2_apply.at(n))

            def layer_scores(n, layer, side, g):
                def source(c):
                    return x_nat[:, side, c, 0:D] if layer == 0 else normed[:, c, :]
                if layer == 0:
                    dve.wait_ge(x0_ready.sem, x0_ready.at(g))
                token_dots(source, attn_row[:, layer, 0, :], attn_row[:, layer, 1, :],
                           bias_col[:, 0, layer:layer + 1], 0.0 if layer == 0 else bias_col[:, 1, layer:layer + 1],
                           s_i, s_j).then_inc(s_ready.sem, 1)
                dve.wait_ge(s_ready.sem, s_ready.at(n))

            def final_norm(g, n, side):
                dve.wait_ge(x_ready.sem, x_ready.at(n))
                norm_stats(lambda c: x_res[:, side, c, :], lng_chain, g)

            def final_apply(g, side):
                norm_apply(lambda c: x_res[:, side, c, :], lng_rstd, g, lng_apply)

            def final_mask(g, side):
                dve.tensor_copy(mask_g[:, :, :], mask_t[:, side, :, :]).then_inc(mask_g_ready.sem, 1)
                dve.wait_ge(mask_g_ready.sem, mask_g_ready.at(g, 1))
                for c in range(NC):
                    last = dve.tensor_copy(mask_g[:, c, c * P:(c + 1) * P], diag_t[:, side, c, :])
                last.then_inc(mask_g_ready.sem, 1)
                dve.wait_ge(mask_g_ready.sem, mask_g_ready.at(g, 2))

            def final_bounded(g, n):
                dve.wait_ge(g_low.sem, g_low.at(g))
                dve.wait_ge(g_rows.sem, g_rows.at(g))
                dve.tensor_scalar(sg_j8[:, :], wh[:, :, D + 1], 1.0 - SLOPE, None, ALU.mult).then_inc(sg_scaled.sem, 1)
                dve.wait_ge(sg_scaled.sem, sg_scaled.at(g))
                dve.wait_ge(agg_done.sem, agg_done.at(n))
                def scores(j):
                    dve.scalar_tensor_tensor(out=probs[:, j, :], in0=ps_a[1][:, :], scalar=sg_j8[:, j:j + 1],
                                             in1=low_sb[:, :], op0=ALU.add, op1=ALU.max).then_inc(g_q.sem, 1)

                def negate(j):
                    dve.wait_ge(g_max.sem, g_max.at(g, j + 1))
                    dve.tensor_scalar(col_neg[:, j:j + 1], col_max[:, j:j + 1], -1.0, None, ALU.mult).then_inc(g_neg.sem, 1)

                scores(0)
                for j in range(NC):
                    dve.wait_ge(g_q.sem, g_q.at(g, j + 1))
                    if j + 1 < NC:
                        scores(j + 1)
                    else:
                        negate(j - 1)
                    dve.tensor_tensor_reduce(probs[:, j, :], probs[:, j, :], mask_g[:, j, :], 1.0,
                                             -3e38, ALU.add, ALU.max, col_max[:, j:j + 1]).then_inc(g_max.sem, 1)
                    if 1 <= j < NC - 1:
                        negate(j - 1)
                negate(NC - 1)

            def final_scale(g):
                dve.wait_ge(g_exp.sem, g_exp.at(g))
                dve.reciprocal(col_r[:, :], col_sum[:, :]).then_inc(g_r.sem, 1)
                dve.wait_ge(g_r.sem, g_r.at(g))
                for c in range(NC):
                    last = dve.tensor_scalar(wh[:, c, 0:D], wh[:, c, 0:D], col_r[:, c:c + 1], None, ALU.mult)
                last.then_inc(wh_scaled.sem, 1)

            def final_leaky(g, chunks):
                for c in chunks:
                    dve.wait_ge(o_done.sem, o_done.at(g, c + 1))
                    if c >= 2:
                        dve.wait_ge(o_ready.sem, o_ready.at(g, c - 1))
                    dve.tensor_scalar(o_tmp[:, c % 2, :], ps_a[c % 2][:, 0:D], SLOPE, None, ALU.mult).then_inc(o_low.sem, 1)
                    dve.wait_ge(o_low.sem, o_low.at(g, c + 1))
                    dve.tensor_tensor(o_tmp[:, c % 2, :], ps_a[c % 2][:, 0:D], o_tmp[:, c % 2, :],
                                      ALU.max).then_inc(o_leaky.sem, 1)

            def parts(i):
                dve.wait_ge(weights_in[i % 2].sem, weights_in[i % 2].at(i // 2))
                _, hi, lo, _, _ = weight_loads[i]
                dve.tensor_copy(hi, staged(i)).then_inc(split_w.sem, 1)
                dve.wait_ge(split_w.sem, split_w.at(2 * i))
                dve.tensor_tensor(lo, staged(i), hi.bitcast(F32), ALU.subtract).then_inc(split_w.sem, 1)

            dve.wait_ge(loaded.sem, loaded.at(SMALL - 1))
            dve.wait_ge(consts.sem, consts.at(2))
            count = [0]

            def step(instruction):
                instruction.then_inc(setup_v.sem, 1)
                count[0] += 1
                dve.wait_ge(setup_v.sem, setup_v.at(count[0] - 1))

            step(dve.tensor_copy(ones_r[:, :], ones_f))
            step(dve.tensor_copy(ident_r[:, :], ident[:, :]))
            step(dve.tensor_copy(b2_round, b2_two))
            step(dve.scalar_tensor_tensor(out=b2_parts[:, :, :], in0=b2_round.bitcast(F32),
                                          scalar=minus_row[:, 0:1], in1=b2_two, op0=ALU.mult, op1=ALU.add))
            for l in range(1, LAYERS):
                for t in range(2):
                    step(dve.tensor_tensor_reduce(junk[:, 0:D], attn_row[:, l, t, :], beta2_row[:, l - 1, :], 1.0,
                                                  bias_col[:, 0, l:l + 1] if t == 0 else 0.0, ALU.mult, ALU.add,
                                                  bias_col[:, t, l:l + 1]))
                    step(dve.tensor_tensor(attn_row[:, l, t, :], attn_row[:, l, t, :], g2_row[:, l - 1, :], ALU.mult))

            for k in range(KC):
                for t in range(2):
                    step(dve.tensor_tensor_reduce(junk[:, D:2 * D], w_last[:, k, 0:D], a_row[:, t, :], 1.0, 0.0, ALU.mult,
                                                  ALU.add, w_last[:, k, D + t:D + t + 1]))
            assert count[0] == SETUP

            prepare_masks(0, 0)
            prepare_x(0, 0, 0)
            layer_scores(0, 0, 0, 0)
            for i in range(len(weight_loads)):
                parts(i)
            dve.wait_ge(split_w.sem, split_w.at(2 * len(weight_loads) - 1))
            neighbour_max(0, 0)
            bounded_scores(0, 0)
            attention_sum(0, 0)
            attention_norm(0)
            h_rest(0)
            prepare_masks(1, 1)

            def pair_body(pair, first, last):
                for n, side, layer, final, prepare, attend, layer_a in slots(pair, first, last):
                    other = 1 - side
                    graph_a = pair * 2 + 1 if side == 0 else pair * 2 + 2
                    late = pair * 2 - 2 + side if layer == 0 and not first else None
                    if side == 0 and late is not None:
                        final_mask(final, 1)
                    if not (first and side == 0 and layer == 0):
                        ff_norm(n - 1)
                    if attend and layer_a == 0:
                        prepare_x(graph_a, other, pair + side, n)
                    if late is not None and side == 0:
                        final_scale(late)
                    if attend:
                        layer_scores(n + 1, layer_a, other, graph_a)
                    if not (attend and layer_a == 0):
                        gelu_rest(n, 1)
                    if final is not None and late is None:
                        gelu_rest(n, 3)
                    if late is not None and side == 1:
                        final_scale(late)
                    if late is not None and side == 0:
                        gelu_rest(n, 3)
                        final_leaky(late, range(NC))
                    if late is not None and side == 1:
                        final_leaky(late, (0, 1))
                    if attend:
                        neighbour_max(n + 1, other)
                    if late is not None and side == 1:
                        final_leaky(late, (2, 3))
                    if final is None:
                        gelu_rest(n, 3)
                    if final is not None:
                        final_norm(final, n - 1, other)
                    if attend:
                        bounded_scores(n + 1, other, late)
                    if final is not None:
                        final_apply(final, other)
                    gelu_rest(n, 4)
                    if layer == LAST and side == 0:
                        final_mask(pair * 2, 0)
                    if prepare is not None:
                        prepare_masks(prepare, side)
                    if attend:
                        attention_sum(n + 1, other)
                        attention_norm(n + 1)
                    if final is not None:
                        final_bounded(final, n + 1 if attend else n)
                    if attend:
                        h_rest(n + 1)

            each_pair(dve, pair_body)
            final_mask(B - 1, 1)
            ff_norm(B * LAYERS - 1)
            final_scale(B - 2)
            final_leaky(B - 2, range(NC))
            final_norm(B - 1, B * LAYERS - 1, 1)
            final_apply(B - 1, 1)
            final_bounded(B - 1, B * LAYERS - 1)
            final_scale(B - 1)
            final_leaky(B - 1, range(NC))

        @block.gpsimd
        def _(pool):
            def inverse_root(chain, idx, done):
                pool.wait_ge(chain.sem, chain.at(idx))
                pool.tensor_tensor(rstd[:, :], var_eps[:, :], minus_half[:, :], ALU.pow).then_inc(done.sem, 1)

            def layer_input(n, side, layer, step=None):
                pool.wait_ge(ln2_apply.sem, ln2_apply.at(n))
                row = g2_row[:, layer:layer + 1, :].broadcast_to([P, NC, D])
                if layer < LAST:
                    target = x_nat[:, side, :, 0:D]
                    pool.tensor_tensor(target, normed[:, :, :], row, ALU.mult).then_inc(x_scaled.sem, 1)
                    pool.wait_ge(x_scaled.sem, x_scaled.at(n))
                    shift = beta2_row[:, layer:layer + 1, :].broadcast_to([P, NC, D])
                    pool.tensor_tensor(target, target, shift, ALU.add).then_inc(x_ready.sem, 1)
                else:
                    pool.tensor_tensor(normed[:, :, :], normed[:, :, :], row, ALU.mult).then_inc(x_scaled.sem, 1)
                    if step is not None:
                        gelu_rest(step, 2)
                    pool.wait_ge(x_scaled.sem, x_scaled.at(n))
                    pool.tensor_tensor(x_res[:, side, :, :], x_res[:, side, :, :], normed[:, :, :],
                                       ALU.add).then_inc(x_ready.sem, 1)

            def residual_shift(pair, side):
                g = pair * 2 + side
                pool.wait_ge(res_loaded[side].sem, res_loaded[side].at(pair))
                row = beta2_row[:, LAST:LAST + 1, :].broadcast_to([P, NC, D])
                pool.tensor_tensor(x_res[:, side, :, :], x_res[:, side, :, :], row, ALU.add).then_inc(res_beta.sem, 1)
                pool.wait_ge(res_beta.sem, res_beta.at(g))

            def gelu_rest(n, f):
                pool.wait_ge(gelu_done.sem, gelu_done.at(n, f + 1))
                pool.tensor_tensor(gelu_lo[:, f % RING, :], g_full[:, f % 2, :],
                                   gelu_hi[:, f % RING, :].bitcast(F32), ALU.subtract).then_inc(lo_done[0].sem, 1)

            def mask_scores(n, side):
                for j in range(POOL_MASKED):
                    pool.wait_ge(q_ready.sem, q_ready.at(n, j + 1))
                    pool.tensor_tensor(probs[:, j, :], probs[:, j, :], mask_t[:, side, j, :],
                                       ALU.add).then_inc(q_masked[0].sem, 1)

            def final_add(g, side):
                for c in range(NC):
                    pool.wait_ge(o_leaky.sem, o_leaky.at(g, c + 1))
                    pool.tensor_tensor(x_res[:, side, c, :], x_res[:, side, c, :], o_tmp[:, c % 2, :],
                                       ALU.add).then_inc(o_ready.sem, 1)

            pool.memset(ident[:, :], 0.0)
            pool.memset(ones_f, 1.0)
            pool.memset(minus_half[:, :], -0.5)
            pool.memset(minus_row[:, :], -1.0)
            pool.memset(x_nat[:, :, :, D:D + 1], 1.0).then_inc(consts.sem, 1)
            pool.wait_ge(consts.sem, consts.at(0))
            pool.affine_select(out=minus_row[:, :], in_=minus_row[:, :], compare_op=ALU.not_equal, fill=0.0,
                               base=0, pattern=[[0, 1]], channel_multiplier=1)
            pool.affine_select(out=ident[:, :], in_=ident[:, :], compare_op=ALU.not_equal, fill=1.0,
                               base=0, pattern=[[-1, P]], channel_multiplier=1).then_inc(consts.sem, 1)
            pool.wait_ge(consts.sem, consts.at(1))
            pool.tensor_copy(ident_b[:, :], ident[:, :]).then_inc(consts.sem, 1)
            inverse_root(ln0_chain, 0, ln0_rstd)
            mask_scores(0, 0)
            inverse_root(ln1_chain, 0, ln1_rstd)

            def pair_body(pair, first, last):
                for n, side, layer, final, prepare, attend, layer_a in slots(pair, first, last):
                    other = 1 - side
                    graph_a = pair * 2 + 1 if side == 0 else pair * 2 + 2
                    late = pair * 2 - 2 + side if layer == 0 and not first else None
                    begins = first and side == 0 and layer == 0
                    if not begins:
                        inverse_root(ln2_chain, n - 1, ln2_rstd)
                    gelu_rest(n, 0)
                    if attend and layer_a == 0:
                        inverse_root(ln0_chain, graph_a, ln0_rstd)
                    if final is not None:
                        layer_input(n - 1, other, LAST, n)
                    else:
                        if not begins:
                            layer_input(n - 1, other, layer - 1 + side)
                        gelu_rest(n, 2)
                    if late is not None:
                        final_add(late, side)
                    if final is not None:
                        inverse_root(lng_chain, final, lng_rstd)
                    if attend:
                        mask_scores(n + 1, other)
                    gelu_rest(n, 5)
                    gelu_rest(n, 6)
                    if layer == LAST:
                        residual_shift(pair, side)
                    if attend:
                        inverse_root(ln1_chain, n + 1, ln1_rstd)
                    gelu_rest(n, 7)

            each_pair(pool, pair_body)
            inverse_root(ln2_chain, B * LAYERS - 1, ln2_rstd)
            final_add(B - 2, 0)
            layer_input(B * LAYERS - 1, 1, LAST)
            inverse_root(lng_chain, B - 1, lng_rstd)
            final_add(B - 1, 1)


_INS = ["x", "adj", "L0_gnn_attn_w", "L0_gnn_attn_b", "L0_gnn_W1", "L0_gnn_b1", "L0_gnn_W2", "L0_gnn_b2",
        "L0_gnn_g1", "L0_gnn_beta1", "L0_gnn_g2", "L0_gnn_beta2", "L1_gnn_W", "L1_gnn_a"]


def kernel(**inputs):
    import numpy as np
    import concourse.bacc as bacc
    from concourse.bass_utils import run_bass_kernel_spmd

    nc = bacc.Bacc("TRN2", target_bir_lowering=False, num_devices=1)
    arrays, args = {}, []
    for name in _INS:
        array = np.ascontiguousarray(inputs[name])
        arrays[f"{name}_dram"] = array
        args.append(nc.dram_tensor(f"{name}_dram", array.shape, mybir.dt.from_np(array.dtype),
                                   kind="ExternalInput").ap())
    out = nc.dram_tensor("out_dram", arrays["x_dram"].shape, F32, kind="ExternalOutput").ap()
    gnn_program(nc, *args, out)
    result = run_bass_kernel_spmd(nc, [arrays], core_ids=[0])
    return result.results[0]["out_dram"]
```

```python
from contextlib import ExitStack

import concourse.bass as bass
from concourse import mybir

F32 = mybir.dt.float32
F32R = mybir.dt.float32r
BF16 = mybir.dt.bfloat16
I32 = mybir.dt.int32
ALU = mybir.AluOpType
ACT = mybir.ActivationFunctionType

P = 128
EPS = 1e-5
SLOPE = 0.2
MASKED = -1e30



class Counted:

    def __init__(self, sem, per, unit):
        self.sem, self.per, self.unit = sem, per, unit

    def at(self, step, k=None):
        return step * (self.per * self.unit) + (self.per if k is None else k) * self.unit


def begun(value):
    return not isinstance(value, int) or value > 0


def gnn_program(nc, x, adj, attn_w, attn_b, W1, b1, W2, b2, g1, beta1, g2, beta2, Wl, al, out):
    B, N, D = x.shape
    LAYERS, _, F = W1.shape
    NC = N // P
    KC = D // P
    FC = F // P
    STEPS = 2 * LAYERS
    PAIRS = B // 2
    RING = 3
    LAST = LAYERS - 1
    BY_VECTOR = (1, 3, 4)
    BY_POOL = tuple(f for f in range(FC) if f not in BY_VECTOR)

    def lo_turn(f):
        return (1, BY_VECTOR.index(f) + 1) if f in BY_VECTOR else (0, BY_POOL.index(f) + 1)

    with ExitStack() as ctx:
        def sb(name, shape, dt):
            return ctx.enter_context(nc.sbuf_tensor(name, shape, dt))

        def sem(name, per=1, unit=1):
            return Counted(ctx.enter_context(nc.semaphore(name)), per, unit)

        w1_hi = sb("w1_hi", [P, LAYERS, KC, F], F32R)
        w1_lo = sb("w1_lo", [P, LAYERS, KC, F], F32R)
        w2_hi = sb("w2_hi", [P, LAYERS, FC, D], F32R)
        w2_lo = sb("w2_lo", [P, LAYERS, FC, D], F32R)
        w_last = sb("w_last", [P, KC, D + 2], F32)
        VECS = LAYERS * (FC + 2 * KC)
        vec_col = sb("vec_col", [P, VECS], F32)
        b1_col = vec_col[:, 0:LAYERS * FC].rearrange("p (l c) -> p l c", l=LAYERS)
        g1_col = vec_col[:, LAYERS * FC:LAYERS * (FC + KC)].rearrange("p (l c) -> p l c", l=LAYERS)
        beta1_col = vec_col[:, LAYERS * (FC + KC):VECS].rearrange("p (l c) -> p l c", l=LAYERS)
        attn_row = sb("attn_row", [P, LAYERS, 2, D], F32)
        g2_row = sb("g2_row", [P, LAYERS, D], F32)
        beta2_row = sb("beta2_row", [P, LAYERS, D], F32)
        bias_col = sb("bias_col", [P, 2, LAYERS], F32)
        b2_parts = sb("b2_parts", [2, LAYERS, D], F32R)
        minus_row = sb("minus_row", [2, 1], F32)
        ones_r = sb("ones_r", [2, P], F32R)
        ident = sb("ident", [P, P], F32)
        ident_r = sb("ident_r", [P, P], F32R)
        ident_b = sb("ident_b", [P, P], BF16)
        minus_half = sb("minus_half", [P, NC], F32)
        x_nat = sb("x_nat", [P, 2, NC, D + 1], F32)
        h_hi = sb("h_hi", [P, KC, N], F32R)
        h_lo = sb("h_lo", [P, KC, N], F32R)
        mask_nat = sb("mask_nat", [P, 2, NC, N], BF16)
        mask_t = sb("mask_t", [P, 2, NC, N], BF16)
        diag_t = sb("diag_t", [P, 2, NC, P], BF16)
        diag_nat = sb("diag_nat", [P, NC, P], BF16)
        adj_in = sb("adj_in", [P, 2, N], I32)
        adj_self = sb("adj_self", [P, P], F32)
        x_res = sb("x_res", [P, 2, NC, D], F32)
        mask_g = sb("mask_g", [P, NC, N], BF16)
        probs = sb("probs", [P, NC, N], F32)
        g_full = sb("g_full", [P, 2, N], F32)
        gelu_hi = sb("gelu_hi", [P, RING, N], F32R)
        gelu_lo = sb("gelu_lo", [P, RING, N], F32R)
        normed = sb("normed", [P, NC, D], F32)
        wh = sb("wh", [P, NC, D + 2], F32)
        h_last = sb("h_last", [P, KC, N], F32)
        stats = sb("stats", [P, NC, 6], F32)
        mean_sum = sb("mean_sum", [P, NC], F32)
        mean_gap = sb("mean_gap", [P, NC], F32)
        squares = sb("squares", [P, NC], F32)
        gap_sq = sb("gap_sq", [P, NC], F32)
        mean = sb("mean", [P, NC], F32)
        var_eps = sb("var_eps", [P, NC], F32)
        rstd = sb("rstd", [P, NC], F32)
        s_i = sb("s_i", [P, NC], F32)
        s_j = sb("s_j", [P, NC], F32)
        s_j8 = sb("s_j8", [P, NC], F32)
        s_j2 = sb("s_j2", [P, NC], F32)
        s_max = sb("s_max", [P, NC], F32)
        sg_j8 = sb("sg_j8", [P, NC], F32)
        x0_shift = sb("x0_shift", [P, NC], F32)
        o_tmp = sb("o_tmp", [P, 2, D], F32)
        low_sb = sb("low_sb", [P, N], F32)
        top = sb("top", [P, NC], F32)
        high = sb("high", [P, NC], F32)
        low = sb("low", [P, NC], F32)
        r_sum = sb("r_sum", [P, NC], F32)
        col_max = sb("col_max", [P, NC], F32)
        col_neg = sb("col_neg", [P, NC], F32)
        col_sum = sb("col_sum", [P, NC], F32)
        col_r = sb("col_r", [P, NC], F32)

        h_full = h_last
        junk = h_last[:, :, :].rearrange("p k n -> p (k n)").bitcast(BF16)
        vec_rows = o_tmp[0:VECS, 0, 0:P]
        a_row = normed[:, 0:2, :]
        b2_two = wh[0:2, 0:LAYERS, 0:D]
        ones_f = wh[0:2, LAYERS, 0:P]
        b2_round = h_last[0:2, :, :].rearrange("p k n -> p (k n)")[:, 0:LAYERS * D].bitcast(F32R).rearrange(
            "p (l d) -> p l d", l=LAYERS)

        def bank(name):
            return ctx.enter_context(nc.psum_tensor(name, [P, 512], F32))

        ps_u = [bank("ps_u0"), bank("ps_u1")]
        ps_d = [bank("ps_d0"), bank("ps_d1")]
        ps_a = [bank("ps_a0"), bank("ps_a1")]
        ps_t = [bank("ps_t0"), bank("ps_t1")]

        loaded = sem("loaded", 1, 16)
        weights_in = [sem(f"weights_in{i}", 1, 16) for i in range(2)]
        consts = sem("consts")
        w_high = sem("w_high")
        w_low = sem("w_low")
        vec_tr = sem("vec_tr")
        vec_ready = sem("vec_ready")
        setup_v = sem("setup_v")
        x_loaded = [sem(f"x_loaded{side}", 1, 16) for side in range(2)]
        adj_loaded = [sem(f"adj_loaded{i}", NC // 2, 16) for i in range(2)]
        ln0_chain = sem("ln0_chain", 4)
        ln0_rstd = sem("ln0_rstd")
        ln0_shift = sem("ln0_shift")
        x0_ready = sem("x0_ready")
        self_added = sem("self_added", NC)
        nat_ready = sem("nat_ready", NC)
        mask_pe = sem("mask_pe", NC + 1)
        mask_ready = sem("mask_ready", NC + 1)
        s_ready = sem("s_ready")
        sj_bc = sem("sj_bc")
        max_ready = sem("max_ready")
        row_chain = sem("row_chain", 3)
        rows_bc = sem("rows_bc", 2)
        low_ready = sem("low_ready")
        q_ready = sem("q_ready", NC)
        q_masked = [sem("q_masked0", NC // 2), sem("q_masked1", NC // 2)]
        p_ready = sem("p_ready", NC)
        agg_done = sem("agg_done", NC)
        rsum_ready = sem("rsum_ready", NC)
        y_ready = sem("y_ready", NC)
        ln1_chain = sem("ln1_chain", 4)
        ln1_rstd = sem("ln1_rstd")
        ln1_apply = sem("ln1_apply", NC)
        h_tr = sem("h_tr", KC)
        hi_ready = sem("hi_ready", KC)
        h_act = sem("h_act", KC)
        h_ready = sem("h_ready", KC)
        u_done = sem("u_done", FC)
        gelu_done = sem("gelu_done", FC)
        hi0_done = sem("hi0_done")
        lo_done = [sem("lo_done0", len(BY_POOL)), sem("lo_done1", len(BY_VECTOR))]
        d_used = sem("d_used", FC - 1)
        d_done = sem("d_done", 2)
        ln2_chain = sem("ln2_chain", 4)
        ln2_rstd = sem("ln2_rstd")
        ln2_apply = sem("ln2_apply", 2)
        x_scaled = sem("x_scaled")
        x_ready = sem("x_ready")
        res_loaded = [sem(f"res_loaded{side}", 1, 16) for side in range(2)]
        res_beta = sem("res_beta")
        lng_chain = sem("lng_chain", 4)
        lng_rstd = sem("lng_rstd")
        lng_apply = sem("lng_apply", NC)
        g_tr = sem("g_tr", KC)
        g_act = sem("g_act", KC)
        wh_done = sem("wh_done", NC)
        wh_copy = sem("wh_copy", NC)
        sg_scaled = sem("sg_scaled")
        mask_g_ready = sem("mask_g_ready", 2)
        g_rows = sem("g_rows")
        g_low = sem("g_low")
        g_q = sem("g_q", NC)
        g_max = sem("g_max", NC)
        g_neg = sem("g_neg", NC)
        g_exp = sem("g_exp", NC)
        g_r = sem("g_r")
        wh_scaled = sem("wh_scaled")
        o_done = sem("o_done", NC)
        o_low = sem("o_low", NC)
        o_leaky = sem("o_leaky", NC)
        o_ready = sem("o_ready", NC)
        stored = [sem(f"stored{side}", NC, 16) for side in range(2)]

        block = ctx.enter_context(nc.Block())

        stage = [probs[:, :, :].rearrange("p c n -> p (c n)"), x_res[:, :, :, :].rearrange("p s c d -> p (s c d)")]
        weight_loads = []
        for l in range(LAYERS):
            weight_loads.append((W1[l].rearrange("(k p) f -> p k f", p=P), w1_hi[:, l], w1_lo[:, l], KC, F))
            weight_loads.append((W2[l].rearrange("(k p) f -> p k f", p=P), w2_hi[:, l], w2_lo[:, l], FC, D))
        SETUP = 4 + 4 * (LAYERS - 1) + 2 * KC
        SMALL = 10

        def staged(i):
            _, _, _, k, n = weight_loads[i]
            return stage[min(i, 1)][:, 0:k * n].rearrange("p (k n) -> p k n", k=k)

        def each_pair(engine, body):
            body(0, True, PAIRS == 1)
            if PAIRS > 2:
                with engine.Fori(1, PAIRS - 1) as pair:
                    body(pair, False, False)
            if PAIRS > 1:
                body(PAIRS - 1, False, True)

        def slots(pair, first, last):
            for layer in range(LAYERS):
                for side in range(2):
                    n = pair * STEPS + 2 * layer + side
                    final = None
                    if side == 1 and layer == LAST:
                        final = pair * 2
                    if side == 0 and layer == 0 and not first:
                        final = pair * 2 - 1
                    prepare = pair * 2 + 2 + side if layer == LAST and not last else None
                    attend = not (side == 1 and layer == LAST and last)
                    yield n, side, layer, final, prepare, attend, (layer + side) % LAYERS

        @block.sync
        def _(sp):
            small = [
                (vec_rows[0:LAYERS * FC, :], b1.rearrange("l (c p) -> (l c) p", p=P)),
                (vec_rows[LAYERS * FC:LAYERS * (FC + KC), :], g1.rearrange("l (c p) -> (l c) p", p=P)),
                (vec_rows[LAYERS * (FC + KC):VECS, :], beta1.rearrange("l (c p) -> (l c) p", p=P)),
                (attn_row[:, :, :, :], attn_w.rearrange("(o l) (t d) -> o l t d", o=1, t=2).broadcast_to([P, LAYERS, 2, D])),
                (w_last[:, :, 0:D], Wl.rearrange("(k p) f -> p k f", p=P)),
                (a_row, al.rearrange("(t d) o -> o t d", t=2).broadcast_to([P, 2, D])),
                (g2_row[:, :, :], g2.rearrange("(o l) d -> o l d", o=1).broadcast_to([P, LAYERS, D])),
                (beta2_row[:, :, :], beta2.rearrange("(o l) d -> o l d", o=1).broadcast_to([P, LAYERS, D])),
                (b2_two, b2.rearrange("(o l) d -> o l d", o=1).broadcast_to([2, LAYERS, D])),
                (bias_col[:, 0, :], attn_b.rearrange("(o l) -> o l", o=1).broadcast_to([P, LAYERS])),
            ]
            assert len(small) == SMALL

            def load_weights(i):
                if i >= 2:
                    sp.wait_ge(w_low.sem, w_low.at(i - 1))
                sp.dma_start(staged(i), weight_loads[i][0]).then_inc(weights_in[i % 2].sem, 16)

            def load_input(g, side, step_before):
                if step_before is not None:
                    sp.wait_ge(y_ready.sem, y_ready.at(step_before))
                sp.dma_start(x_nat[:, side, :, 0:D], x[g].rearrange("(c p) d -> p c d", p=P)).then_inc(x_loaded[side].sem, 16)
                load_adjacency(g, range(NC))

            def load_adjacency(g, chunks):
                for c in chunks:
                    if begun(self_added.at(g, c - 1)):
                        sp.wait_ge(self_added.sem, self_added.at(g, c - 1))
                    sp.dma_start(adj_in[:, c % 2, :], adj[g][c * P:(c + 1) * P, :]).then_inc(adj_loaded[c % 2].sem, 16)

            def load_residual(pair, side):
                g = pair * 2 + side
                if begun(stored[side].at(pair - 1)):
                    sp.wait_ge(stored[side].sem, stored[side].at(pair - 1))
                sp.dma_start(x_res[:, side, :, :], x[g].rearrange("(c p) d -> p c d", p=P)).then_inc(res_loaded[side].sem, 16)

            def store(g, side):
                for c in range(NC):
                    sp.wait_ge(o_ready.sem, o_ready.at(g, c + 1))
                    sp.dma_start(out[g][c * P:(c + 1) * P, :], x_res[:, side, c, :]).then_inc(stored[side].sem, 16)

            load_adjacency(0, (0, 1))
            sp.wait_ge(consts.sem, consts.at(0))
            sp.dma_start(x_nat[:, 0, :, 0:D], x[0].rearrange("(c p) d -> p c d", p=P)).then_inc(x_loaded[0].sem, 16)
            load_adjacency(0, (2, 3))
            for dst, src in small:
                sp.dma_start(dst, src).then_inc(loaded.sem, 16)
            load_weights(0)
            load_weights(1)
            load_input(1, 1, None)

            def pair_body(pair, first, last):
                for n, side, layer, final, prepare, attend, _ in slots(pair, first, last):
                    if layer == 0 and not first:
                        store(pair * 2 - 2 + side, side)
                    if first and n + 2 < len(weight_loads):
                        load_weights(n + 2)
                    if layer == LAST:
                        if first and side == 0:
                            sp.wait_ge(w_low.sem, w_low.at(len(weight_loads) - 1))
                        load_residual(pair, side)
                    if prepare is not None:
                        load_input(prepare, side, n)

            each_pair(sp, pair_body)
            for side in range(2):
                store(B - 2 + side, side)
            for side in range(2):
                sp.wait_ge(stored[side].sem, stored[side].at(PAIRS - 1))

        @block.tensor
        def _(pe):
            def columns_to_rows(dst, col):
                for c in range(NC):
                    last = pe.transpose(dst[:, c * P:(c + 1) * P], col[:, c:c + 1].broadcast_to([P, P]),
                                        ident[:, :])
                return last

            def mask_transposes(g, side, chunks, bank=None):
                for c in chunks:
                    view = (ps_t[c % 2] if bank is None else bank)[:, :].bitcast(BF16)
                    if c >= 2:
                        pe.wait_ge(mask_ready.sem, mask_ready.at(g, c - 1))
                    if c < NC:
                        pe.wait_ge(nat_ready.sem, nat_ready.at(g, c + 1))
                    for j in range(NC):
                        block = mask_nat[:, side, c, j * P:(j + 1) * P] if c < NC else diag_nat[:, j, :]
                        last = pe.transpose(view[:, j * P:(j + 1) * P], block, ident_b[:, :])
                    last.then_inc(mask_pe.sem, 1)

            def scores_row(n):
                pe.wait_ge(s_ready.sem, s_ready.at(n))
                columns_to_rows(ps_t[0], s_j).then_inc(sj_bc.sem, 1)

            def bound_rows(n):
                pe.wait_ge(row_chain.sem, row_chain.at(n))
                columns_to_rows(ps_t[0], low).then_inc(rows_bc.sem, 1)
                columns_to_rows(ps_t[1], high).then_inc(rows_bc.sem, 1)

            def attend_out(n, side, layer, g, late):
                if layer == 0:
                    pe.wait_ge(x0_ready.sem, x0_ready.at(g))
                else:
                    pe.wait_ge(x_ready.sem, x_ready.at(n - 2))
                for c in range(NC):
                    if c >= 2:
                        pe.wait_ge(y_ready.sem, y_ready.at(n, c - 1))
                    elif late is not None:
                        pe.wait_ge(o_leaky.sem, o_leaky.at(late, NC - 1 + c))
                    elif begun(y_ready.at(n - 1)):
                        pe.wait_ge(y_ready.sem, y_ready.at(n - 1))
                    for j in range(NC):
                        if c == 0:
                            pe.wait_ge(p_ready.sem, p_ready.at(n, j + 1))
                        last = pe.matmul(ps_a[c % 2][:, 0:D + 1], probs[:, j, c * P:(c + 1) * P], x_nat[:, side, j, :],
                                         start=(j == 0), stop=(j == NC - 1))
                    last.then_inc(agg_done.sem, 1)

            def turn_tokens(source, applied, turned, step):
                for c in range(NC):
                    pe.wait_ge(applied.sem, applied.at(step, c + 1))
                    for k in range(KC):
                        last = pe.transpose(ps_t[k][:, c * P:(c + 1) * P], source[:, c, k * P:(k + 1) * P], ident[:, :])
                        if c == NC - 1:
                            last.then_inc(turned.sem, 1)

            def up_first(n, layer):
                for k in range(KC):
                    pe.wait_ge(hi_ready.sem, hi_ready.at(n, k + 1))
                    for f in range(2):
                        if k == 0 and begun(gelu_done.at(n, f - 1)):
                            pe.wait_ge(gelu_done.sem, gelu_done.at(n, f - 1))
                        lhs = slice(f * P, (f + 1) * P)
                        pe.matmul(ps_u[f][:, :], w1_hi[:, layer, k, lhs], h_hi[:, k, :], start=(k == 0), stop=False)
                        pe.matmul(ps_u[f][:, :], w1_lo[:, layer, k, lhs], h_hi[:, k, :], start=False, stop=False)
                for f in range(2):
                    lhs = slice(f * P, (f + 1) * P)
                    for k in range(KC):
                        pe.wait_ge(h_ready.sem, h_ready.at(n, k + 1))
                        last = pe.matmul(ps_u[f][:, :], w1_hi[:, layer, k, lhs], h_lo[:, k, :],
                                         start=False, stop=(k == KC - 1))
                    last.then_inc(u_done.sem, 1)

            def up(n, layer, f):
                pe.wait_ge(gelu_done.sem, gelu_done.at(n, f - 1))
                lhs = slice(f * P, (f + 1) * P)
                terms = [(w, h, k) for k in range(KC) for w, h in ((w1_hi, h_hi), (w1_hi, h_lo), (w1_lo, h_hi))]
                for i, (w, h, k) in enumerate(terms):
                    last = pe.matmul(ps_u[f % 2][:, :], w[:, layer, k, lhs], h[:, k, :],
                                     start=(i == 0), stop=(i == len(terms) - 1))
                last.then_inc(u_done.sem, 1)

            def residual(n, layer):
                for c in range(NC):
                    if c % 2 == 0 and begun(ln2_apply.at(n - 1)):
                        pe.wait_ge(ln2_apply.sem, ln2_apply.at(n - 1, c // 2 + 1))
                    cols = (c % 2) * D
                    dst = ps_d[c // 2]
                    for k in range(KC):
                        for i, h in enumerate((h_hi, h_lo)):
                            pe.matmul(dst[:, cols + k * P:cols + (k + 1) * P], h[:, k, c * P:(c + 1) * P],
                                      ident_r[:, :], start=(c % 2 == 0 and k == 0 and i == 0), stop=False,
                                      skip_group_check=True)
                    pe.matmul(dst[:, cols:cols + D], ones_r[:, :], b2_parts[:, layer, :], start=False, stop=False,
                              skip_group_check=True)

            def down(n, layer, f):
                if f == 0:
                    residual(n, layer)
                by, turn = lo_turn(f)
                pe.wait_ge(lo_done[by].sem, lo_done[by].at(n, turn))
                r = f % RING
                for c in range(NC):
                    cols = (c % 2) * D
                    tok = slice(c * P, (c + 1) * P)
                    for i, (h, w) in enumerate(((gelu_hi, w2_hi), (gelu_hi, w2_lo), (gelu_lo, w2_hi))):
                        last = pe.matmul(ps_d[c // 2][:, cols:cols + D], h[:, r, tok], w[:, layer, f, :],
                                         start=False, stop=(f == FC - 1 and i == 2), skip_group_check=True)
                    if f == FC - 1 and c % 2 == 1:
                        last.then_inc(d_done.sem, 1)
                    if f < FC - 1 and c == NC - 1:
                        last.then_inc(d_used.sem, 1)

            def project(g, n):
                pe.wait_ge(g_act.sem, g_act.at(g))
                for c in range(NC):
                    if c >= 2:
                        pe.wait_ge(wh_copy.sem, wh_copy.at(g, c - 1))
                    else:
                        pe.wait_ge(y_ready.sem, y_ready.at(n, NC - 1 + c))
                    for k in range(KC):
                        last = pe.matmul(ps_a[c % 2][:, 0:D + 2], h_last[:, k, c * P:(c + 1) * P], w_last[:, k, :],
                                         start=(k == 0), stop=(k == KC - 1))
                    last.then_inc(wh_done.sem, 1)

            def final_rows(g):
                pe.wait_ge(wh_copy.sem, wh_copy.at(g))
                columns_to_rows(ps_a[1], wh[:, :, D]).then_inc(g_rows.sem, 1)

            def final_out(g, chunks):
                pe.wait_ge(wh_scaled.sem, wh_scaled.at(g))
                for c in chunks:
                    if c >= 2:
                        pe.wait_ge(o_leaky.sem, o_leaky.at(g, c - 1))
                    for j in range(NC):
                        last = pe.matmul(ps_a[c % 2][:, 0:D], probs[:, j, c * P:(c + 1) * P], wh[:, j, 0:D],
                                         start=(j == 0), stop=(j == NC - 1))
                    last.then_inc(o_done.sem, 1)

            pe.wait_ge(consts.sem, consts.at(2))
            mask_transposes(0, 0, range(NC + 1))
            pe.wait_ge(mask_ready.sem, mask_ready.at(0, NC + 1))
            scores_row(0)
            bound_rows(0)
            pe.wait_ge(loaded.sem, loaded.at(SMALL - 1))
            pe.transpose(ps_u[0][:, 0:VECS], vec_rows, ident[0:VECS, 0:VECS]).then_inc(vec_tr.sem, 1)
            attend_out(0, 0, 0, 0, None)
            mask_transposes(1, 1, range(NC + 1))
            pe.wait_ge(mask_ready.sem, mask_ready.at(1, NC + 1))
            turn_tokens(normed, ln1_apply, h_tr, 0)
            pe.wait_ge(setup_v.sem, setup_v.at(SETUP - 1))

            def regular_slot(n, side, layer, late, prepare, graph_a, layer_a):
                up_first(n, layer)
                up(n, layer, 2)
                up(n, layer, 3)
                down(n, layer, 0)
                pe.wait_ge(h_act.sem, h_act.at(n))
                if late is None:
                    scores_row(n + 1)
                down(n, layer, 1)
                up(n, layer, 4)
                if late is not None:
                    scores_row(n + 1)
                    final_out(late, range(NC))
                down(n, layer, 2)
                bound_rows(n + 1)
                up(n, layer, 5)
                down(n, layer, 3)
                up(n, layer, 6)
                attend_out(n + 1, 1 - side, layer_a, graph_a, late)
                pe.wait_ge(q_ready.sem, q_ready.at(n + 1))
                down(n, layer, 4)
                if prepare is not None:
                    mask_transposes(prepare, 0, (0, 1))
                up(n, layer, 7)
                if prepare is not None:
                    mask_transposes(prepare, 0, (2, 3))
                down(n, layer, 5)
                if prepare is not None:
                    pe.wait_ge(y_ready.sem, y_ready.at(n + 1))
                    mask_transposes(prepare, 0, (4,), ps_a[0])
                    pe.wait_ge(mask_ready.sem, mask_ready.at(prepare, NC))
                turn_tokens(normed, ln1_apply, h_tr, n + 1)
                down(n, layer, 6)
                down(n, layer, 7)

            def final_slot(n, side, layer, final, late, attend, graph_a, layer_a):
                up_first(n, layer)
                pe.wait_ge(h_act.sem, h_act.at(n))
                up(n, layer, 2)
                up(n, layer, 3)
                if late is not None:
                    mask_transposes(graph_a, 1, (0, 1))
                down(n, layer, 0)
                down(n, layer, 1)
                up(n, layer, 4)
                if late is not None:
                    mask_transposes(graph_a, 1, (2, 3))
                    final_out(late, (0, 1))
                    mask_transposes(graph_a, 1, (4,))
                down(n, layer, 2)
                if late is not None:
                    final_out(late, (2, 3))
                    pe.wait_ge(mask_ready.sem, mask_ready.at(graph_a, NC + 1))
                    scores_row(n + 1)
                if attend and late is None:
                    scores_row(n + 1)
                up(n, layer, 5)
                down(n, layer, 3)
                if attend:
                    bound_rows(n + 1)
                up(n, layer, 6)
                down(n, layer, 4)
                up(n, layer, 7)
                if attend:
                    attend_out(n + 1, 1 - side, layer_a, graph_a, late)
                turn_tokens(wh, lng_apply, g_tr, final)
                down(n, layer, 5)
                project(final, n + 1 if attend else n)
                final_rows(final)
                if attend:
                    turn_tokens(normed, ln1_apply, h_tr, n + 1)
                down(n, layer, 6)
                down(n, layer, 7)

            def pair_body(pair, first, last):
                for n, side, layer, final, prepare, attend, layer_a in slots(pair, first, last):
                    graph_a = pair * 2 + 1 if side == 0 else pair * 2 + 2
                    late = pair * 2 - 2 + side if layer == 0 and not first else None
                    if first and side == 0:
                        pe.wait_ge(w_high.sem, w_high.at(2 * layer + 1))
                        pe.wait_ge(w_low.sem, w_low.at(2 * layer + 1))
                    if final is None:
                        regular_slot(n, side, layer, late, prepare if side == 0 else None, graph_a, layer_a)
                    else:
                        final_slot(n, side, layer, final, late, attend, graph_a, layer_a)

            each_pair(pe, pair_body)
            final_out(B - 2, range(NC))
            turn_tokens(wh, lng_apply, g_tr, B - 1)
            pe.wait_ge(o_leaky.sem, o_leaky.at(B - 2))
            project(B - 1, B * LAYERS - 1)
            final_rows(B - 1)
            final_out(B - 1, range(NC))

        @block.scalar
        def _(act):
            def mask_copies(g, side, chunks, bank=None):
                if begun(mask_g_ready.at(g - 2)):
                    act.wait_ge(mask_g_ready.sem, mask_g_ready.at(g - 2))
                for c in chunks:
                    act.wait_ge(mask_pe.sem, mask_pe.at(g, c + 1))
                    src = (ps_t[c % 2] if bank is None else bank)[:, :].bitcast(BF16)[:, 0:N].rearrange("p (j i) -> p j i", i=P)
                    dst = mask_t[:, side, :, c * P:(c + 1) * P] if c < NC else diag_t[:, side, :, :]
                    act.activation(dst, src, ACT.Copy).then_inc(mask_ready.sem, 1)

            def input_apply(g, side):
                act.wait_ge(ln0_shift.sem, ln0_shift.at(g))
                for c in range(NC):
                    last = act.activation(x_nat[:, side, c, 0:D], x_nat[:, side, c, 0:D], ACT.Relu,
                                          bias=x0_shift[:, c:c + 1], scale=rstd[:, c:c + 1])
                last.then_inc(x0_ready.sem, 1)

            def low_row(n):
                act.wait_ge(rows_bc.sem, rows_bc.at(n, 1))
                act.activation(low_sb[:, :], ps_t[0][:, :], ACT.Copy).then_inc(low_ready.sem, 1)

            def exps(n):
                for j in range(NC):
                    act.wait_ge(q_masked[j % 2].sem, q_masked[j % 2].at(n, j // 2 + 1))
                    act.activation(probs[:, j, :], probs[:, j, :], ACT.Exp, bias=s_j2[:, j:j + 1]).then_inc(p_ready.sem, 1)

            def h_split(n, layer):
                for k in range(KC):
                    act.wait_ge(h_tr.sem, h_tr.at(n, k + 1))
                    act.activation(h_hi[:, k, :], ps_t[k][:, :], ACT.Identity,
                                   bias=beta1_col[:, layer, k:k + 1], scale=g1_col[:, layer, k:k + 1]).then_inc(hi_ready.sem, 1)
                    act.activation(h_full[:, k, :], ps_t[k][:, :], ACT.Identity, bias=beta1_col[:, layer, k:k + 1],
                                   scale=g1_col[:, layer, k:k + 1]).then_inc(h_act.sem, 1)

            def gelu(n, layer, f):
                act.wait_ge(u_done.sem, u_done.at(n, f + 1))
                by, turn = lo_turn((f - 2) % FC)
                step = n if f >= 2 else n - 1
                if begun(lo_done[by].at(step, turn)):
                    act.wait_ge(lo_done[by].sem, lo_done[by].at(step, turn))
                full = act.activation(g_full[:, f % 2, :], ps_u[f % 2][:, :], ACT.Gelu, bias=b1_col[:, layer, f:f + 1])
                if f == 0:
                    full.then_inc(gelu_done.sem, 1)
                    return
                if f >= RING:
                    act.wait_ge(d_used.sem, d_used.at(n, f - RING + 1))
                act.activation(gelu_hi[:, f % RING, :], ps_u[f % 2][:, :], ACT.Gelu,
                               bias=b1_col[:, layer, f:f + 1]).then_inc(gelu_done.sem, 1)

            def final_h(g):
                for k in range(KC):
                    act.wait_ge(g_tr.sem, g_tr.at(g, k + 1))
                    act.activation(h_last[:, k, :], ps_t[k][:, :], ACT.Relu).then_inc(g_act.sem, 1)

            def final_wh(g):
                for c in range(NC):
                    act.wait_ge(wh_done.sem, wh_done.at(g, c + 1))
                    act.activation(wh[:, c, :], ps_a[c % 2][:, 0:D + 2], ACT.Copy).then_inc(wh_copy.sem, 1)

            def final_low(g):
                act.wait_ge(g_rows.sem, g_rows.at(g))
                act.activation(low_sb[:, :], ps_a[1][:, :], ACT.Copy, scale=SLOPE).then_inc(g_low.sem, 1)

            def final_exps(g):
                for j in range(NC):
                    act.wait_ge(g_neg.sem, g_neg.at(g, j + 1))
                    act.activation(probs[:, j, :], probs[:, j, :], ACT.Exp, bias=col_neg[:, j:j + 1],
                                   accum_out=col_sum[:, j:j + 1]).then_inc(g_exp.sem, 1)

            def high_part(i):
                act.wait_ge(weights_in[i % 2].sem, weights_in[i % 2].at(i // 2))
                act.activation(weight_loads[i][1], staged(i), ACT.Copy).then_inc(w_high.sem, 1)

            mask_copies(0, 0, range(NC + 1))
            input_apply(0, 0)
            high_part(0)
            high_part(1)
            low_row(0)
            act.wait_ge(vec_tr.sem, vec_tr.at(0))
            act.activation(vec_col[:, :], ps_u[0][:, 0:VECS], ACT.Copy).then_inc(vec_ready.sem, 1)
            exps(0)
            mask_copies(1, 1, range(NC + 1))
            act.wait_ge(vec_ready.sem, vec_ready.at(0))
            h_split(0, 0)

            def pair_body(pair, first, last):
                for n, side, layer, final, prepare, attend, layer_a in slots(pair, first, last):
                    late = pair * 2 - 2 + side if layer == 0 and not first else None
                    masks_y = pair * 2 + 1 if side == 0 and late is not None else None
                    masks_x = prepare if side == 0 else None
                    gelu(n, layer, 0)
                    gelu(n, layer, 1)
                    gelu(n, layer, 2)
                    if late is not None:
                        final_exps(late)
                    if masks_y is not None:
                        mask_copies(masks_y, 1, (0, 1))
                    if masks_y is not None:
                        mask_copies(masks_y, 1, (2, 3))
                    if attend and layer_a == 0:
                        input_apply(pair * 2 + 1 + side, 1 - side)
                    gelu(n, layer, 3)
                    if first and n + 2 < len(weight_loads):
                        high_part(n + 2)
                    gelu(n, layer, 4)
                    if masks_y is not None:
                        mask_copies(masks_y, 1, (4,))
                    if final is not None:
                        gelu(n, layer, 5)
                    if attend:
                        low_row(n + 1)
                        exps(n + 1)
                    if final is None:
                        gelu(n, layer, 5)
                    gelu(n, layer, 6)
                    if final is not None:
                        final_h(final)
                    if masks_x is not None:
                        mask_copies(masks_x, 0, (0, 1))
                    gelu(n, layer, 7)
                    if masks_x is not None:
                        mask_copies(masks_x, 0, (2, 3))
                    if final is not None:
                        final_wh(final)
                        final_low(final)
                    if masks_x is not None:
                        mask_copies(masks_x, 0, (4,), ps_a[0])
                    if attend:
                        h_split(n + 1, layer_a)

            each_pair(act, pair_body)
            final_exps(B - 2)
            final_h(B - 1)
            final_wh(B - 1)
            final_low(B - 1)
            final_exps(B - 1)

        @block.vector
        def _(dve):
            def norm_stats(source, chain, idx):
                for c in range(NC):
                    last = dve.bn_stats(stats[:, c, :], source(c))
                last.then_inc(chain.sem, 1)
                variance(chain, idx)

            def variance(chain, idx):
                dve.wait_ge(chain.sem, chain.at(idx, 1))
                dve.tensor_tensor(mean_sum[:, :], stats[:, :, 1], stats[:, :, 4], ALU.add)
                dve.tensor_tensor(mean_gap[:, :], stats[:, :, 1], stats[:, :, 4], ALU.subtract)
                dve.scalar_tensor_tensor(out=squares[:, :], in0=stats[:, :, 2], scalar=D * EPS,
                                         in1=stats[:, :, 5], op0=ALU.add, op1=ALU.add).then_inc(chain.sem, 1)
                dve.wait_ge(chain.sem, chain.at(idx, 2))
                dve.tensor_scalar(mean[:, :], mean_sum[:, :], 0.5, None, ALU.mult)
                dve.scalar_tensor_tensor(out=gap_sq[:, :], in0=mean_gap[:, :], scalar=0.25,
                                         in1=mean_gap[:, :], op0=ALU.mult, op1=ALU.mult).then_inc(chain.sem, 1)
                dve.wait_ge(chain.sem, chain.at(idx, 3))
                dve.scalar_tensor_tensor(out=var_eps[:, :], in0=squares[:, :], scalar=1.0 / D,
                                         in1=gap_sq[:, :], op0=ALU.mult, op1=ALU.add).then_inc(chain.sem, 1)

            def prepare_masks(g, side, chunks):
                for c in chunks:
                    blk = slice(c * P, (c + 1) * P)
                    dve.wait_ge(adj_loaded[c % 2].sem, adj_loaded[c % 2].at(g, c // 2 + 1))
                    dve.tensor_scalar(mask_nat[:, side, c, :], adj_in[:, c % 2, :], 0.0, MASKED, ALU.is_le, ALU.mult)
                    dve.tensor_scalar(diag_nat[:, c, :], adj_in[:, c % 2, blk], 0.0, MASKED, ALU.is_le, ALU.mult)
                    dve.tensor_tensor(adj_self[:, :], adj_in[:, c % 2, blk], ident[:, :], ALU.add).then_inc(self_added.sem, 1)
                    dve.wait_ge(self_added.sem, self_added.at(g, c + 1))
                    dve.tensor_scalar(mask_nat[:, side, c, blk], adj_self[:, :], 0.0, MASKED,
                                      ALU.is_le, ALU.mult).then_inc(nat_ready.sem, 1)
                    dve.wait_ge(nat_ready.sem, nat_ready.at(g, c + 1))

            def prepare_x(g, side, pair, meanwhile=None, late=None):
                dve.wait_ge(x_loaded[side].sem, x_loaded[side].at(pair))
                norm_stats(lambda c: x_nat[:, side, c, 0:D], ln0_chain, g)
                if meanwhile is not None:
                    gelu_rest(meanwhile, 1)
                if late is not None:
                    final_scale(late)
                dve.wait_ge(ln0_rstd.sem, ln0_rstd.at(g))
                dve.scalar_tensor_tensor(out=x0_shift[:, :], in0=mean[:, :], scalar=-1.0, in1=rstd[:, :],
                                         op0=ALU.mult, op1=ALU.mult).then_inc(ln0_shift.sem, 1)

            def token_dots(source, row_i, row_j, init_i, init_j, to_i, to_j):
                for c in range(NC):
                    dve.tensor_tensor_reduce(junk[:, 2 * c * D:(2 * c + 1) * D], source(c), row_i, 1.0, init_i,
                                             ALU.mult, ALU.add, to_i[:, c:c + 1])
                    last = dve.tensor_tensor_reduce(junk[:, (2 * c + 1) * D:(2 * c + 2) * D], source(c), row_j, 1.0,
                                                    init_j, ALU.mult, ALU.add, to_j[:, c:c + 1])
                return last

            def neighbour_max(n, side):
                dve.wait_ge(sj_bc.sem, sj_bc.at(n))
                dve.tensor_scalar(s_j8[:, :], s_j[:, :], 1.0 - SLOPE, None, ALU.mult)
                dve.tensor_scalar(s_j2[:, :], s_j[:, :], SLOPE, None, ALU.mult)
                for c in range(NC):
                    last = dve.tensor_tensor_reduce(junk[:, c * N:(c + 1) * N], ps_t[0][:, :], mask_nat[:, side, c, :],
                                                    1.0, -3e38, ALU.add, ALU.max, s_max[:, c:c + 1])
                last.then_inc(max_ready.sem, 1)
                dve.wait_ge(max_ready.sem, max_ready.at(n))
                dve.tensor_tensor(high[:, :], s_i[:, :], s_max[:, :], ALU.add).then_inc(row_chain.sem, 1)
                dve.wait_ge(row_chain.sem, row_chain.at(n, 1))
                dve.scalar_tensor_tensor(out=top[:, :], in0=high[:, :], scalar=SLOPE, in1=high[:, :],
                                         op0=ALU.mult, op1=ALU.max).then_inc(row_chain.sem, 1)
                dve.wait_ge(row_chain.sem, row_chain.at(n, 2))
                dve.tensor_tensor(high[:, :], s_i[:, :], top[:, :], ALU.subtract)
                dve.scalar_tensor_tensor(out=low[:, :], in0=s_i[:, :], scalar=SLOPE, in1=top[:, :],
                                         op0=ALU.mult, op1=ALU.subtract).then_inc(row_chain.sem, 1)

            def bounded_scores(n, side, graph_before=None):
                dve.wait_ge(low_ready.sem, low_ready.at(n))
                dve.wait_ge(rows_bc.sem, rows_bc.at(n))
                if begun(agg_done.at(n - 1)):
                    dve.wait_ge(agg_done.sem, agg_done.at(n - 1))
                if graph_before is not None:
                    dve.wait_ge(o_done.sem, o_done.at(graph_before))
                def masked(j):
                    dve.wait_ge(q_ready.sem, q_ready.at(n, j + 1))
                    dve.tensor_tensor(probs[:, j, :], probs[:, j, :], mask_t[:, side, j, :],
                                      ALU.add).then_inc(q_masked[1].sem, 1)

                for j in range(NC):
                    dve.scalar_tensor_tensor(out=probs[:, j, :], in0=ps_t[1][:, :], scalar=s_j8[:, j:j + 1],
                                             in1=low_sb[:, :], op0=ALU.add, op1=ALU.max).then_inc(q_ready.sem, 1)
                    if j >= 2 and j % 2 == 0:
                        masked(j - 1)
                masked(NC - 1)

            def attention_sum(n, side, final=None, prepare=None):
                for c in range(NC):
                    dve.wait_ge(agg_done.sem, agg_done.at(n, c + 1))
                    dve.reciprocal(r_sum[:, c:c + 1], ps_a[c % 2][:, D:D + 1]).then_inc(rsum_ready.sem, 1)
                    dve.wait_ge(rsum_ready.sem, rsum_ready.at(n, c + 1))
                    dve.scalar_tensor_tensor(out=normed[:, c, :], in0=ps_a[c % 2][:, 0:D],
                                             scalar=r_sum[:, c:c + 1], in1=x_nat[:, side, c, 0:D],
                                             op0=ALU.mult, op1=ALU.add).then_inc(y_ready.sem, 1)
                    dve.wait_ge(y_ready.sem, y_ready.at(n, c + 1))
                    last = dve.bn_stats(stats[:, c, :], normed[:, c, :])
                    if c == NC - 1:
                        last.then_inc(ln1_chain.sem, 1)
                    if final is not None and 2 * c < NC:
                        final_apply(final, side, (2 * c, 2 * c + 1))
                    if prepare is not None:
                        prepare_masks(prepare, 1 - side, (c,))
                variance(ln1_chain, n)

            def attention_norm(n):
                dve.wait_ge(ln1_rstd.sem, ln1_rstd.at(n))
                for c in range(NC):
                    dve.tensor_scalar(normed[:, c, :], normed[:, c, :], mean[:, c:c + 1], rstd[:, c:c + 1],
                                      ALU.subtract, ALU.mult).then_inc(ln1_apply.sem, 1)
                dve.wait_ge(ln1_apply.sem, ln1_apply.at(n))

            def h_rest(n):
                for k in range(KC):
                    dve.wait_ge(h_act.sem, h_act.at(n, k + 1))
                    dve.tensor_tensor(h_lo[:, k, :], h_full[:, k, :],
                                      h_hi[:, k, :].bitcast(F32), ALU.subtract).then_inc(h_ready.sem, 1)
                dve.wait_ge(h_ready.sem, h_ready.at(n))

            def gelu_high(n):
                dve.wait_ge(gelu_done.sem, gelu_done.at(n, 1))
                dve.tensor_copy(gelu_hi[:, 0, :], g_full[:, 0, :]).then_inc(hi0_done.sem, 1)

            def gelu_rest(n, f):
                dve.wait_ge(gelu_done.sem, gelu_done.at(n, f + 1))
                dve.tensor_tensor(gelu_lo[:, f % RING, :], g_full[:, f % 2, :],
                                  gelu_hi[:, f % RING, :].bitcast(F32), ALU.subtract).then_inc(lo_done[1].sem, 1)

            def ff_norm(n, meanwhile=()):
                def source(c):
                    return ps_d[c // 2][:, (c % 2) * D:(c % 2 + 1) * D]
                for c in range(NC):
                    if c % 2 == 0:
                        dve.wait_ge(d_done.sem, d_done.at(n, c // 2 + 1))
                    last = dve.bn_stats(stats[:, c, :], source(c))
                last.then_inc(ln2_chain.sem, 1)
                variance(ln2_chain, n)
                if 0 in meanwhile:
                    gelu_high(n + 1)
                if 1 in meanwhile:
                    gelu_rest(n + 1, 1)
                dve.wait_ge(ln2_rstd.sem, ln2_rstd.at(n))
                for c in range(NC):
                    last = dve.tensor_scalar(normed[:, c, :], source(c), mean[:, c:c + 1], rstd[:, c:c + 1],
                                             ALU.subtract, ALU.mult)
                    if c % 2 == 1:
                        last.then_inc(ln2_apply.sem, 1)
                dve.wait_ge(ln2_apply.sem, ln2_apply.at(n))

            def layer_scores(n, layer, side, g):
                def source(c):
                    return x_nat[:, side, c, 0:D] if layer == 0 else normed[:, c, :]
                if layer == 0:
                    dve.wait_ge(x0_ready.sem, x0_ready.at(g))
                token_dots(source, attn_row[:, layer, 0, :], attn_row[:, layer, 1, :],
                           bias_col[:, 0, layer:layer + 1], 0.0 if layer == 0 else bias_col[:, 1, layer:layer + 1],
                           s_i, s_j).then_inc(s_ready.sem, 1)
                dve.wait_ge(s_ready.sem, s_ready.at(n))

            def final_norm(g, n, side):
                dve.wait_ge(x_ready.sem, x_ready.at(n))
                norm_stats(lambda c: x_res[:, side, c, :], lng_chain, g)

            def final_apply(g, side, chunks):
                dve.wait_ge(lng_rstd.sem, lng_rstd.at(g))
                for c in chunks:
                    dve.tensor_scalar(wh[:, c, 0:D], x_res[:, side, c, :], mean[:, c:c + 1], rstd[:, c:c + 1],
                                      ALU.subtract, ALU.mult).then_inc(lng_apply.sem, 1)
                if c == NC - 1:
                    dve.wait_ge(lng_apply.sem, lng_apply.at(g))

            def final_mask(g, side):
                dve.tensor_copy(mask_g[:, :, :], mask_t[:, side, :, :]).then_inc(mask_g_ready.sem, 1)
                dve.wait_ge(mask_g_ready.sem, mask_g_ready.at(g, 1))
                for c in range(NC):
                    last = dve.tensor_copy(mask_g[:, c, c * P:(c + 1) * P], diag_t[:, side, c, :])
                last.then_inc(mask_g_ready.sem, 1)
                dve.wait_ge(mask_g_ready.sem, mask_g_ready.at(g, 2))

            def final_bounded(g, first_chunk):
                def scores(j):
                    dve.scalar_tensor_tensor(out=probs[:, j, :], in0=ps_a[1][:, :], scalar=sg_j8[:, j:j + 1],
                                             in1=low_sb[:, :], op0=ALU.add, op1=ALU.max).then_inc(g_q.sem, 1)

                def greatest(j):
                    dve.tensor_tensor_reduce(probs[:, j, :], probs[:, j, :], mask_g[:, j, :], 1.0,
                                             -3e38, ALU.add, ALU.max, col_max[:, j:j + 1]).then_inc(g_max.sem, 1)

                def negate(j):
                    dve.wait_ge(g_max.sem, g_max.at(g, j + 1))
                    dve.tensor_scalar(col_neg[:, j:j + 1], col_max[:, j:j + 1], -1.0, None, ALU.mult).then_inc(g_neg.sem, 1)

                scores(first_chunk)
                dve.wait_ge(g_q.sem, g_q.at(g, first_chunk + 1))
                scores(first_chunk + 1)
                greatest(first_chunk)
                dve.wait_ge(g_q.sem, g_q.at(g, first_chunk + 2))
                negate(first_chunk)
                greatest(first_chunk + 1)
                negate(first_chunk + 1)

            def final_begin(g, n):
                dve.wait_ge(g_low.sem, g_low.at(g))
                dve.wait_ge(g_rows.sem, g_rows.at(g))
                dve.tensor_scalar(sg_j8[:, :], wh[:, :, D + 1], 1.0 - SLOPE, None, ALU.mult).then_inc(sg_scaled.sem, 1)
                dve.wait_ge(sg_scaled.sem, sg_scaled.at(g))
                dve.wait_ge(agg_done.sem, agg_done.at(n))
                final_bounded(g, 0)

            def final_scale(g):
                dve.wait_ge(g_exp.sem, g_exp.at(g))
                dve.reciprocal(col_r[:, :], col_sum[:, :]).then_inc(g_r.sem, 1)
                dve.wait_ge(g_r.sem, g_r.at(g))
                for c in range(NC):
                    last = dve.tensor_scalar(wh[:, c, 0:D], wh[:, c, 0:D], col_r[:, c:c + 1], None, ALU.mult)
                last.then_inc(wh_scaled.sem, 1)

            def final_leaky(g, chunks):
                for c in chunks:
                    dve.wait_ge(o_done.sem, o_done.at(g, c + 1))
                    if c >= 2:
                        dve.wait_ge(o_ready.sem, o_ready.at(g, c - 1))
                    dve.tensor_scalar(o_tmp[:, c % 2, :], ps_a[c % 2][:, 0:D], SLOPE, None, ALU.mult).then_inc(o_low.sem, 1)
                    dve.wait_ge(o_low.sem, o_low.at(g, c + 1))
                    dve.tensor_tensor(o_tmp[:, c % 2, :], ps_a[c % 2][:, 0:D], o_tmp[:, c % 2, :],
                                      ALU.max).then_inc(o_leaky.sem, 1)

            dve.wait_ge(consts.sem, consts.at(2))
            prepare_masks(0, 0, range(NC))
            prepare_x(0, 0, 0)
            dve.wait_ge(loaded.sem, loaded.at(SMALL - 1))
            layer_scores(0, 0, 0, 0)
            neighbour_max(0, 0)
            count = [0]

            def step(instruction):
                instruction.then_inc(setup_v.sem, 1)
                count[0] += 1
                dve.wait_ge(setup_v.sem, setup_v.at(count[0] - 1))

            step(dve.tensor_copy(ones_r[:, :], ones_f))
            step(dve.tensor_copy(ident_r[:, :], ident[:, :]))
            step(dve.tensor_copy(b2_round, b2_two))
            step(dve.scalar_tensor_tensor(out=b2_parts[:, :, :], in0=b2_round.bitcast(F32),
                                          scalar=minus_row[:, 0:1], in1=b2_two, op0=ALU.mult, op1=ALU.add))
            dve.wait_ge(w_high.sem, w_high.at(0))
            dve.wait_ge(w_low.sem, w_low.at(0))
            bounded_scores(0, 0)
            for l in range(1, LAYERS):
                for t in range(2):
                    step(dve.tensor_tensor_reduce(junk[:, 0:D], attn_row[:, l, t, :], beta2_row[:, l - 1, :], 1.0,
                                                  bias_col[:, 0, l:l + 1] if t == 0 else 0.0, ALU.mult, ALU.add,
                                                  bias_col[:, t, l:l + 1]))
                    step(dve.tensor_tensor(attn_row[:, l, t, :], attn_row[:, l, t, :], g2_row[:, l - 1, :], ALU.mult))

            for k in range(KC):
                for t in range(2):
                    step(dve.tensor_tensor_reduce(junk[:, D:2 * D], w_last[:, k, 0:D], a_row[:, t, :], 1.0, 0.0, ALU.mult,
                                                  ALU.add, w_last[:, k, D + t:D + t + 1]))
            assert count[0] == SETUP

            attention_sum(0, 0, prepare=1)
            attention_norm(0)
            h_rest(0)

            def pair_body(pair, first, last):
                for n, side, layer, final, prepare, attend, layer_a in slots(pair, first, last):
                    other = 1 - side
                    graph_a = pair * 2 + 1 if side == 0 else pair * 2 + 2
                    late = pair * 2 - 2 + side if layer == 0 and not first else None
                    if not (first and side == 0 and layer == 0):
                        ff_norm(n - 1, (0,) if late is None else (0, 1))
                    else:
                        gelu_high(n)
                    if late is not None:
                        final_bounded(late, 2)
                    if side == 0 and late is not None:
                        final_mask(final, 1)
                    if attend and layer_a == 0:
                        prepare_x(graph_a, other, pair + side, n if late is None else None, late)
                    if prepare is not None and side == 1:
                        prepare_masks(prepare, side, (0, 1))
                    if attend:
                        layer_scores(n + 1, layer_a, other, graph_a)
                    if not (attend and layer_a == 0) and late is None:
                        gelu_rest(n, 1)
                    if final is not None and late is None:
                        gelu_rest(n, 3)
                    if late is not None and side == 1:
                        final_scale(late)
                    if late is not None and side == 0:
                        gelu_rest(n, 3)
                        final_leaky(late, range(NC))
                    if attend:
                        neighbour_max(n + 1, other)
                    if late is not None and side == 1:
                        final_leaky(late, range(NC))
                    if final is None:
                        gelu_rest(n, 3)
                    gelu_rest(n, 4)
                    if attend:
                        bounded_scores(n + 1, other, late)
                    if layer == LAST and side == 0:
                        final_mask(pair * 2, 0)
                    if final is not None:
                        final_norm(final, n - 1, other)
                    if attend:
                        attention_sum(n + 1, other, final, prepare if side == 0 else None)
                        attention_norm(n + 1)
                    else:
                        final_apply(final, other, range(NC))
                    if prepare is not None and side == 1:
                        prepare_masks(prepare, side, (2, 3))
                    if final is not None:
                        final_begin(final, n + 1 if attend else n)
                    if attend:
                        h_rest(n + 1)

            each_pair(dve, pair_body)
            ff_norm(B * LAYERS - 1)
            final_bounded(B - 2, 2)
            final_mask(B - 1, 1)
            final_scale(B - 2)
            final_norm(B - 1, B * LAYERS - 1, 1)
            final_leaky(B - 2, range(NC))
            final_apply(B - 1, 1, range(NC))
            final_begin(B - 1, B * LAYERS - 1)
            final_bounded(B - 1, 2)
            final_scale(B - 1)
            dve.wait_ge(o_ready.sem, o_ready.at(B - 2))
            final_leaky(B - 1, range(NC))

        @block.gpsimd
        def _(pool):
            def inverse_root(chain, idx, done):
                pool.wait_ge(chain.sem, chain.at(idx))
                pool.tensor_tensor(rstd[:, :], var_eps[:, :], minus_half[:, :], ALU.pow).then_inc(done.sem, 1)

            def layer_input(n, side, layer, step=None):
                pool.wait_ge(ln2_apply.sem, ln2_apply.at(n))
                row = g2_row[:, layer:layer + 1, :].broadcast_to([P, NC, D])
                if layer < LAST:
                    target = x_nat[:, side, :, 0:D]
                    pool.tensor_tensor(target, normed[:, :, :], row, ALU.mult).then_inc(x_scaled.sem, 1)
                    pool.wait_ge(x_scaled.sem, x_scaled.at(n))
                    shift = beta2_row[:, layer:layer + 1, :].broadcast_to([P, NC, D])
                    pool.tensor_tensor(target, target, shift, ALU.add).then_inc(x_ready.sem, 1)
                else:
                    if step is not None:
                        gelu_rest(step, 2)
                    pool.tensor_tensor(normed[:, :, :], normed[:, :, :], row, ALU.mult).then_inc(x_scaled.sem, 1)
                    pool.wait_ge(x_scaled.sem, x_scaled.at(n))
                    pool.tensor_tensor(x_res[:, side, :, :], x_res[:, side, :, :], normed[:, :, :],
                                       ALU.add).then_inc(x_ready.sem, 1)

            def residual_shift(pair, side):
                g = pair * 2 + side
                pool.wait_ge(res_loaded[side].sem, res_loaded[side].at(pair))
                row = beta2_row[:, LAST:LAST + 1, :].broadcast_to([P, NC, D])
                pool.tensor_tensor(x_res[:, side, :, :], x_res[:, side, :, :], row, ALU.add).then_inc(res_beta.sem, 1)
                pool.wait_ge(res_beta.sem, res_beta.at(g))

            def gelu_rest(n, f):
                if f == 0:
                    pool.wait_ge(hi0_done.sem, hi0_done.at(n))
                else:
                    pool.wait_ge(gelu_done.sem, gelu_done.at(n, f + 1))
                pool.tensor_tensor(gelu_lo[:, f % RING, :], g_full[:, f % 2, :],
                                   gelu_hi[:, f % RING, :].bitcast(F32), ALU.subtract).then_inc(lo_done[0].sem, 1)

            def mask_scores(n, side):
                for j in range(0, NC, 2):
                    pool.wait_ge(q_ready.sem, q_ready.at(n, j + 1))
                    pool.tensor_tensor(probs[:, j, :], probs[:, j, :], mask_t[:, side, j, :],
                                       ALU.add).then_inc(q_masked[0].sem, 1)

            def final_add(g, side):
                for c in range(NC):
                    pool.wait_ge(o_leaky.sem, o_leaky.at(g, c + 1))
                    pool.tensor_tensor(x_res[:, side, c, :], x_res[:, side, c, :], o_tmp[:, c % 2, :],
                                       ALU.add).then_inc(o_ready.sem, 1)

            pool.memset(ident[:, :], 0.0)
            pool.memset(ones_f, 1.0)
            pool.memset(minus_half[:, :], -0.5)
            pool.memset(minus_row[:, :], -1.0)
            pool.memset(x_nat[:, :, :, D:D + 1], 1.0).then_inc(consts.sem, 1)
            pool.wait_ge(consts.sem, consts.at(0))
            pool.affine_select(out=minus_row[:, :], in_=minus_row[:, :], compare_op=ALU.not_equal, fill=0.0,
                               base=0, pattern=[[0, 1]], channel_multiplier=1)
            pool.affine_select(out=ident[:, :], in_=ident[:, :], compare_op=ALU.not_equal, fill=1.0,
                               base=0, pattern=[[-1, P]], channel_multiplier=1).then_inc(consts.sem, 1)
            pool.wait_ge(consts.sem, consts.at(1))
            pool.tensor_copy(ident_b[:, :], ident[:, :]).then_inc(consts.sem, 1)
            def low_part(i):
                pool.wait_ge(w_high.sem, w_high.at(i))
                pool.tensor_tensor(weight_loads[i][2], staged(i), weight_loads[i][1].bitcast(F32),
                                   ALU.subtract).then_inc(w_low.sem, 1)

            inverse_root(ln0_chain, 0, ln0_rstd)
            low_part(0)
            mask_scores(0, 0)
            low_part(1)
            inverse_root(ln1_chain, 0, ln1_rstd)

            def pair_body(pair, first, last):
                for n, side, layer, final, prepare, attend, layer_a in slots(pair, first, last):
                    other = 1 - side
                    graph_a = pair * 2 + 1 if side == 0 else pair * 2 + 2
                    late = pair * 2 - 2 + side if layer == 0 and not first else None
                    begins = first and side == 0 and layer == 0
                    if not begins:
                        inverse_root(ln2_chain, n - 1, ln2_rstd)
                    gelu_rest(n, 0)
                    if attend and layer_a == 0:
                        inverse_root(ln0_chain, graph_a, ln0_rstd)
                    if final is not None:
                        layer_input(n - 1, other, LAST, n)
                    else:
                        if not begins:
                            layer_input(n - 1, other, layer - 1 + side)
                        gelu_rest(n, 2)
                    if late is not None:
                        final_add(late, side)
                    if attend:
                        mask_scores(n + 1, other)
                    if final is not None:
                        inverse_root(lng_chain, final, lng_rstd)
                    gelu_rest(n, 5)
                    gelu_rest(n, 6)
                    if first and n + 2 < len(weight_loads):
                        low_part(n + 2)
                    if layer == LAST:
                        residual_shift(pair, side)
                    if attend:
                        inverse_root(ln1_chain, n + 1, ln1_rstd)
                    gelu_rest(n, 7)

            each_pair(pool, pair_body)
            inverse_root(ln2_chain, B * LAYERS - 1, ln2_rstd)
            layer_input(B * LAYERS - 1, 1, LAST)
            inverse_root(lng_chain, B - 1, lng_rstd)
            final_add(B - 2, 0)
            final_add(B - 1, 1)


_INS = ["x", "adj", "L0_gnn_attn_w", "L0_gnn_attn_b", "L0_gnn_W1", "L0_gnn_b1", "L0_gnn_W2", "L0_gnn_b2",
        "L0_gnn_g1", "L0_gnn_beta1", "L0_gnn_g2", "L0_gnn_beta2", "L1_gnn_W", "L1_gnn_a"]


def kernel(**inputs):
    import numpy as np
    import concourse.bacc as bacc
    from concourse.bass_utils import run_bass_kernel_spmd

    nc = bacc.Bacc("TRN2", target_bir_lowering=False, num_devices=1)
    arrays, args = {}, []
    for name in _INS:
        array = np.ascontiguousarray(inputs[name])
        arrays[f"{name}_dram"] = array
        args.append(nc.dram_tensor(f"{name}_dram", array.shape, mybir.dt.from_np(array.dtype),
                                   kind="ExternalInput").ap())
    out = nc.dram_tensor("out_dram", arrays["x_dram"].shape, F32, kind="ExternalOutput").ap()
    gnn_program(nc, *args, out)
    result = run_bass_kernel_spmd(nc, [arrays], core_ids=[0])
    return result.results[0]["out_dram"]
```
